# Optimizing a Trainium2 kernel written in Bass

```python
import numpy as np
import jax
import jax.numpy as jnp

def _softmax(x, axis=-1):
    return jax.nn.softmax(x, axis=axis)

def _gelu(x):
    return jax.nn.gelu(x, approximate=True)

def _silu(x):
    return jax.nn.silu(x)

def _sigmoid(x):
    return jax.nn.sigmoid(x)

def _layernorm(x, axis=-1, eps=1e-05):
    m = jnp.mean(x, axis=axis, keepdims=True)
    v = jnp.var(x, axis=axis, keepdims=True)
    return (x - m) / jnp.sqrt(v + eps)

def _scatter_add(tgt, idx, src, axis=0):
    return tgt.at[idx].add(src)

def _segment_sum(src, seg, n):
    return jax.ops.segment_sum(src, seg, n)
kernel_name = 'mk_gnn_resnorm_d1_gnn_r8_f50dca'

def setup_inputs(seed: int=0):
    np.random.seed(seed)
    _w = jnp.asarray

    def _rec_inputs():
        import jax
        import jax.numpy as jnp
        _gk = jax.random.key(seed)
        x = -0.0001006 + 1 * jax.random.normal(jax.random.fold_in(_gk, 1), (6250, 96), jnp.float32)
        src = jax.random.randint(jax.random.fold_in(_gk, 2), (100000,), 0, 6250, jnp.int32)
        dst = jnp.minimum((6250 * jax.random.uniform(jax.random.fold_in(_gk, 3), (100000,)) ** 2.0).astype(jnp.int32), 49999)
        _o = jnp.argsort(dst, stable=True)
        src = src[_o]
        dst = dst[_o]
        edge_attr_96 = 5.93493e-05 + 1.00006 * jax.random.normal(jax.random.fold_in(_gk, 11), (100000, 96), jnp.float32)
        return (x, src, dst, edge_attr_96)
    x, src, dst, edge_attr_96 = _rec_inputs()

    def _L0_gnn_setup():
        import jax, jax.numpy as jnp
        import numpy as np
        N_NODES = 6250
        N_EDGES = 100000
        IN_DIM = 96
        NUM_HEADS = 8
        HEAD_DIM = IN_DIM // NUM_HEADS
        key = jax.random.key(seed)
        ks = jax.random.split(key, 11)
        s = 1.0 / np.sqrt(IN_DIM)
        return {'x': jax.random.normal(ks[0], (N_NODES, IN_DIM), dtype=jnp.float32), 'edge_index': jax.random.randint(ks[1], (2, N_EDGES), 0, N_NODES, dtype=jnp.int64), 'edge_attr': jax.random.normal(ks[2], (N_EDGES, IN_DIM), dtype=jnp.float32), 'Wq': jax.random.normal(ks[3], (IN_DIM, IN_DIM), dtype=jnp.float32) * s, 'bq': jax.random.normal(ks[4], (IN_DIM,), dtype=jnp.float32) * s, 'Wk': jax.random.normal(ks[5], (IN_DIM, IN_DIM), dtype=jnp.float32) * s, 'bk': jax.random.normal(ks[6], (IN_DIM,), dtype=jnp.float32) * s, 'We': jax.random.normal(ks[7], (IN_DIM, IN_DIM), dtype=jnp.float32) * s, 'be': jax.random.normal(ks[8], (IN_DIM,), dtype=jnp.float32) * s, 'Wv': jax.random.normal(ks[9], (IN_DIM, IN_DIM), dtype=jnp.float32) * s, 'bv': jax.random.normal(ks[10], (IN_DIM,), dtype=jnp.float32) * s}
    _L0_gnn_all = _L0_gnn_setup()
    _L0_gnn_in = {k: v for k, v in _L0_gnn_all.items() if k in ('Wq', 'bq', 'Wk', 'bk', 'We', 'be', 'Wv', 'bv')}
    del _L0_gnn_all
    return {'x': x, 'src': src, 'dst': dst, 'edge_attr_96': edge_attr_96, 'L0_gnn_Wq': _L0_gnn_in['Wq'], 'L0_gnn_bq': _L0_gnn_in['bq'], 'L0_gnn_Wk': _L0_gnn_in['Wk'], 'L0_gnn_bk': _L0_gnn_in['bk'], 'L0_gnn_We': _L0_gnn_in['We'], 'L0_gnn_be': _L0_gnn_in['be'], 'L0_gnn_Wv': _L0_gnn_in['Wv'], 'L0_gnn_bv': _L0_gnn_in['bv']}

def reference(x, src, dst, edge_attr_96, L0_gnn_Wq, L0_gnn_bq, L0_gnn_Wk, L0_gnn_bk, L0_gnn_We, L0_gnn_be, L0_gnn_Wv, L0_gnn_bv):
    import jax
    import jax.numpy as jnp

    def _L0_gnn_ref(x, edge_index, edge_attr, Wq, bq, Wk, bk, We, be, Wv, bv):
        import jax, jax.numpy as jnp
        import numpy as np
        N_NODES = 6250
        N_EDGES = 100000
        IN_DIM = 96
        NUM_HEADS = 8
        HEAD_DIM = IN_DIM // NUM_HEADS
        N = x.shape[0]
        H, D = (NUM_HEADS, HEAD_DIM)
        Q_h = (x @ Wq + bq).reshape(N, H, D)
        K_h = (x @ Wk + bk).reshape(N, H, D)
        V_h = (x @ Wv + bv).reshape(N, H, D)
        E = (edge_attr @ We + be).reshape(-1, H, D)
        src_idx = edge_index[0]
        dst_idx = edge_index[1]
        src = K_h[src_idx]
        dest = Q_h[dst_idx]
        score = src * dest / jnp.sqrt(jnp.asarray(D, x.dtype))
        score = score * E
        score = jnp.exp(jnp.clip(score.sum(-1, keepdims=True), -5.0, 5.0))
        msg = V_h[src_idx] * score
        wV = jax.ops.segment_sum(msg, dst_idx, num_segments=N)
        Z = jax.ops.segment_sum(score, dst_idx, num_segments=N)
        h_out = wV / (Z + 1e-06)
        return h_out.reshape(N, H * D)
    edge_index = jnp.stack([src, dst])
    x = _layernorm(x + _L0_gnn_ref(x, edge_index, edge_attr_96, L0_gnn_Wq, L0_gnn_bq, L0_gnn_Wk, L0_gnn_bk, L0_gnn_We, L0_gnn_be, L0_gnn_Wv, L0_gnn_bv), axis=-1)
    return x

_drawn_inputs = setup_inputs


def setup_inputs(seed=0):
    import zlib

    import numpy as np

    out = dict(_drawn_inputs(seed))
    spreads = {}
    factors = {}
    for name, (base, spread) in spreads.items():
        noise = np.random.default_rng([zlib.crc32(name.encode()), seed]).standard_normal(out[name].shape)
        drawn = base * np.exp(spread * noise) if base else spread * noise
        out[name] = jnp.asarray(drawn.astype(out[name].dtype))
    for name, factor in factors.items():
        out[name] = (out[name] * factor).astype(out[name].dtype)
    return out
```

```python
from contextlib import ExitStack

import numpy as np

import concourse.bass as bass
from concourse import mybir

F32 = mybir.dt.float32
BF16 = mybir.dt.bfloat16
I32 = mybir.dt.int32
U32 = mybir.dt.uint32
ALU = mybir.AluOpType
ACT = mybir.ActivationFunctionType
AX_X = mybir.AxisListType.X

P = 128
N_NODES, N_EDGES = 6250, 100000
HEADS, HEAD_DIM = 8, 12
DIM = HEADS * HEAD_DIM
SUMS = DIM + HEADS
EPS_Z, EPS_NORM, CLIP = 1e-6, 1e-5, 5.0

GROUP_TILES = 4
GROUP = GROUP_TILES * P
GROUPS = -(-N_EDGES // GROUP)
TILES = -(-N_EDGES // P)
EDGES_PADDED = GROUPS * GROUP
PAIRS = GROUPS // 2
WINDOW = 96

NODE_TILES = -(-N_NODES // P)
TABLE_TILES = NODE_TILES + 1
TABLE_ROWS = TABLE_TILES * P
STAGE_TILES = 5
STAGES = TABLE_TILES // STAGE_TILES
SPAN = 512
SPANS = -(-(N_NODES + 1) // SPAN)
ACC_NODES = SPANS * SPAN
FINAL_TILES = 4

KV_RING, EA_RING, REL_RING, QWIN_RING = 6, 3, 3, 4


def tiles_of(group):
    return min(GROUP_TILES, TILES - group * GROUP_TILES)


def build(nc, xT, x_rows, src_cols, dst_cols, dst_rows, eaT, w, b, out):
    assert GROUPS % 2 == 0 and TABLE_TILES % STAGE_TILES == 0
    assert N_NODES + WINDOW <= ACC_NODES and N_NODES + P <= TABLE_ROWS + 1

    kv_table = nc.dram_tensor("kv_table", [TABLE_ROWS, 2 * DIM], F32).ap()
    q_table = nc.dram_tensor("q_table", [TABLE_ROWS, 3 * DIM], BF16).ap()
    rel_rows_dram = nc.dram_tensor("rel_rows_dram", [GROUPS, GROUP], BF16).ap()
    base_dram = nc.dram_tensor("base_dram", [GROUPS], F32).ap()
    span_dram = nc.dram_tensor("span_dram", [GROUPS], F32).ap()

    with ExitStack() as ctx:
        def sb(name, shape, dt):
            return ctx.enter_context(nc.sbuf_tensor(name, shape, dt))

        def psum(name, shape):
            return ctx.enter_context(nc.psum_tensor(name, shape, F32))

        def sem(name):
            return ctx.enter_context(nc.semaphore(name))

        iota_i = sb("iota_i", [P, SPAN], I32)
        iota = sb("iota", [P, SPAN], F32)
        part_i = sb("part_i", [P, 1], I32)
        part_iota = sb("part_iota", [P, 1], F32)
        ident = sb("ident", [P, P], F32)
        eps_norm = sb("eps_norm", [P, 1], F32)

        x_t = sb("x_t", [DIM + 1, TABLE_ROWS], F32)
        w_cat = sb("w_cat", [DIM + 1, 3 * DIM], F32)
        w_e = sb("w_e", [DIM + 1, DIM], F32)
        kv_stage = sb("kv_stage", [P, 2, STAGE_TILES, 2 * DIM], F32)
        q_stage = sb("q_stage", [P, 2, STAGE_TILES, 3 * DIM], BF16)
        q_full = sb("q_full", [P, STAGE_TILES, DIM], F32)
        q_rest = sb("q_rest", [P, STAGE_TILES, DIM], F32)
        q_rest2 = sb("q_rest2", [P, STAGE_TILES, DIM], F32)

        src_idx = sb("src_idx", [P, GROUPS * GROUP_TILES], U32)
        dst_idx = sb("dst_idx", [P, GROUPS * GROUP_TILES], U32)
        dst_f = sb("dst_f", [P, GROUPS * GROUP_TILES], F32)
        rel_f = sb("rel_f", [P, GROUPS * GROUP_TILES], F32)
        base_all = sb("base_all", [P, GROUPS], F32)
        rows_i = sb("rows_i", [PAIRS, 2, GROUP], I32)
        rows_f = sb("rows_f", [PAIRS, 2, GROUP], F32)
        rows_rel = sb("rows_rel", [PAIRS, 2, GROUP], BF16)
        row_min = sb("row_min", [PAIRS, 2], F32)
        row_max = sb("row_max", [PAIRS, 2], F32)
        row_span = sb("row_span", [PAIRS, 2], F32)
        span_row = sb("span_row", [1, GROUPS], F32)
        span_max = sb("span_max", [1, 1], F32)
        base_i = sb("base_i", [1, GROUPS], I32)
        fits_i = sb("fits_i", [1, 1], I32)

        kv = sb("kv", [P, KV_RING, GROUP_TILES, 2 * DIM], F32)
        ea = sb("ea", [DIM + 1, EA_RING, 2 * GROUP], F32)
        rel_bc = sb("rel_bc", [P, REL_RING, 2 * GROUP], BF16)
        q_win = sb("q_win", [P, QWIN_RING, 3 * DIM], BF16)
        pick_t = sb("pick_t", [P, 3, GROUP], BF16)
        pick = sb("pick", [P, 3, GROUP_TILES, WINDOW], F32)
        kq = sb("kq", [P, 2, GROUP_TILES, DIM], F32)
        kqe = sb("kqe", [P, 2, GROUP_TILES, DIM], F32)
        score = sb("score", [P, 2, GROUP_TILES, HEADS], F32)
        clipped = sb("clipped", [P, 2, GROUP_TILES, HEADS], F32)
        msg = sb("msg", [P, 3, GROUP_TILES, SUMS], F32)
        acc_t = sb("acc_t", [SUMS, ACC_NODES], F32)

        g_src = sb("g_src", [P, GROUP_TILES], U32)
        g_dst = sb("g_dst", [P, GROUP_TILES], U32)
        g_dst_f = sb("g_dst_f", [P, GROUP_TILES], F32)
        g_q = sb("g_q", [P, GROUP_TILES, 3 * DIM], BF16)
        g_pick = sb("g_pick", [P, GROUP_TILES, SPAN], F32)

        x_n = sb("x_n", [P, TABLE_TILES, DIM], F32)
        z_inv = sb("z_inv", [P, 2, FINAL_TILES, HEADS], F32)
        z_eps = sb("z_eps", [P, 2, FINAL_TILES, HEADS], F32)
        h = sb("h", [P, 2, FINAL_TILES, DIM], F32)
        mean = sb("mean", [P, 2, FINAL_TILES], F32)
        var = sb("var", [P, 2, FINAL_TILES], F32)
        rstd = sb("rstd", [P, 2, FINAL_TILES], F32)
        sq = sb("sq", [P, 2, FINAL_TILES, DIM], F32)
        y = sb("y", [P, 2, FINAL_TILES, DIM], F32)

        ps_e = [psum(f"ps_e{i}", [P, 512]) for i in range(2)]
        ps_q = [psum(f"ps_q{i}", [P, 512]) for i in range(2)]
        ps_seg = [psum(f"ps_seg{i}", [P, 512]) for i in range(2)]
        ps_table_kv, ps_table_q = ps_e + ps_seg, ps_q
        ps_fin = ps_e

        l_x = [sem(f"l_x{i}") for i in range(STAGES)]
        l_w = sem("l_w")
        l_idx = sem("l_idx")
        l_cols = sem("l_cols")
        l_xn = sem("l_xn")
        c_iota = sem("c_iota")
        c_id0 = sem("c_id0")
        c_ones = sem("c_ones")
        c_iota_f = sem("c_iota_f")
        t_mm = sem("t_mm")
        t_mq = sem("t_mq")
        t_kv = sem("t_kv")
        t_q = sem("t_q")
        t_split = sem("t_split")
        w_kv = [sem(f"w_kv{i}") for i in range(2)]
        w_q = [sem(f"w_q{i}") for i in range(2)]
        r_chain = sem("r_chain")
        r_store = sem("r_store")
        r_rel = sem("r_rel")
        r_load = sem("r_load")
        r_ready = sem("r_ready")
        r_cols = sem("r_cols")
        e_kv = [sem(f"e_kv{i}") for i in range(KV_RING)]
        e_ea = [sem(f"e_ea{i}") for i in range(EA_RING)]
        e_rel = [sem(f"e_rel{i}") for i in range(REL_RING)]
        e_qwin = [sem(f"e_qwin{i}") for i in range(QWIN_RING)]
        e_pt = sem("e_pt")
        e_pick = sem("e_pick")
        e_e = sem("e_e")
        e_q = sem("e_q")
        e_kq = sem("e_kq")
        e_kqe = sem("e_kqe")
        e_sum = sem("e_sum")
        e_clip = sem("e_clip")
        e_exp = sem("e_exp")
        e_msg = sem("e_msg")
        e_seg = sem("e_seg")
        e_acc = sem("e_acc")
        g_free = sem("g_free")
        g_idx = sem("g_idx")
        g_step = sem("g_step")
        g_gather = sem("g_gather")
        g_ea = sem("g_ea")
        g_e = sem("g_e")
        g_clip = sem("g_clip")
        g_exp = sem("g_exp")
        g_pk = sem("g_pk")
        g_seg = sem("g_seg")
        g_chain = sem("g_chain")
        f_acc = sem("f_acc")
        f_tr = sem("f_tr")
        f_div = sem("f_div")
        f_chain = sem("f_chain")
        f_var = sem("f_var")
        f_sqrt = sem("f_sqrt")
        f_cen = sem("f_cen")
        f_sq = sem("f_sq")
        f_y = sem("f_y")
        f_out = [sem(f"f_out{i}") for i in range(2)]

        n_final = -(-NODE_TILES // FINAL_TILES)
        kv_store = kv_table.rearrange("(t p) d -> p t d", p=P)
        q_store = q_table.rearrange("(t p) d -> p t d", p=P)
        w_dram, b_dram = w, b

        def stores(parity, before=None):
            n = 0
            for step in range(parity, n_final if before is None else before, 2):
                first = step * FINAL_TILES
                tiles = min(FINAL_TILES, NODE_TILES - first)
                whole = tiles if (first + tiles) * P <= N_NODES else tiles - 1
                n += (whole > 0) + (whole < tiles)
            return n

        def fits(eng):
            eng.wait_ge(r_ready, 1)
            return eng.value_load(fits_i[0:1, 0:1], min_val=0, max_val=1)

        def base_of(eng, group):
            return eng.value_load(base_i[0:1, group:group + 1], min_val=0, max_val=N_NODES)

        block = ctx.enter_context(nc.Block())

        @block.sync
        def _(sp):
            for i in range(STAGES):
                cols = slice(i * STAGE_TILES * P, (i + 1) * STAGE_TILES * P)
                sp.dma_start(x_t[0:DIM, cols], xT[:, cols]).then_inc(l_x[i], 16)
                if i == 0:
                    for j, name in enumerate("kvq"):
                        sp.dma_start(w_cat[0:DIM, j * DIM:(j + 1) * DIM], w_dram[name]).then_inc(l_w, 16)
                        sp.dma_start(w_cat[DIM:DIM + 1, j * DIM:(j + 1) * DIM],
                                     b_dram[name]).then_inc(l_w, 16)
                    sp.dma_start(w_e[0:DIM, :], w_dram["e"]).then_inc(l_w, 16)
                    sp.dma_start(w_e[DIM:DIM + 1, :], b_dram["e"]).then_inc(l_w, 16)
            for i in range(STAGES):
                rows = slice(i * STAGE_TILES, (i + 1) * STAGE_TILES)
                sp.wait_ge(t_kv, (i + 1) * STAGE_TILES)
                sp.dma_start(kv_store[:, rows, :], kv_stage[:, i % 2]).then_inc(w_kv[i % 2], 16)
                sp.wait_ge(t_split, 5 * (i + 1))
                sp.dma_start(q_store[:, rows, :], q_stage[:, i % 2]).then_inc(w_q[i % 2], 16)
            fit = fits(sp)
            with sp.If(fit == 1):
                for i in range(2):
                    sp.wait_ge(w_q[i], 16 * len(range(i, STAGES, 2)))
                sp.wait_ge(r_rel, 16)
                sp.wait_ge(c_ones, 1)
                rel_pairs = rel_rows_dram.rearrange("(n j) e -> n (j e)", j=2)
                for pair in range(PAIRS):
                    slot, use = pair % EA_RING, pair // EA_RING
                    if use:
                        sp.wait_ge(e_e, 2 * (pair - EA_RING) + 2)
                    sp.dma_start(ea[0:DIM, slot, :], eaT[:, pair * 2 * GROUP:(pair + 1) * 2 * GROUP]
                                 ).then_inc(e_ea[slot], 16)
                    slot, use = pair % REL_RING, pair // REL_RING
                    if use:
                        sp.wait_ge(e_pt, 2 * (pair - REL_RING) + 2)
                    sp.dma_start(rel_bc[:, slot, :], rel_pairs[pair:pair + 1, :].to_broadcast([P, 2 * GROUP])
                                 ).then_inc(e_rel[slot], 16)
                    for group in (2 * pair, 2 * pair + 1):
                        base = base_of(sp, group)
                        slot, use = group % QWIN_RING, group // QWIN_RING
                        if use:
                            sp.wait_ge(e_q, group - QWIN_RING + 1)
                        sp.dma_start(q_win[:, slot, :], q_table[bass.ds(base, P), :]).then_inc(e_qwin[slot], 16)
            with sp.Else():
                sp.wait_ge(c_ones, 1)
                with sp.Fori(0, GROUPS) as group:
                    sp.wait_ge(g_free, group + 1)
                    sp.dma_start(ea[0:DIM, 0, 0:GROUP], eaT[:, bass.ds(group * GROUP, GROUP)]).then_inc(g_ea, 16)
            for step in range(n_final):
                first = step * FINAL_TILES
                n = min(FINAL_TILES, NODE_TILES - first)
                sp.wait_ge(f_y, step + 1)
                whole = n if (first + n) * P <= N_NODES else n - 1
                if whole:
                    sp.dma_start(out[first * P:(first + whole) * P, :].rearrange("(t p) d -> p t d", p=P),
                                 y[:, step % 2, 0:whole, :]).then_inc(f_out[step % 2], 16)
                if whole < n:
                    left = N_NODES - (first + whole) * P
                    sp.dma_start(out[(first + whole) * P:N_NODES, :],
                                 y[0:left, step % 2, whole, :]).then_inc(f_out[step % 2], 16)
            for i in range(2):
                sp.wait_ge(f_out[i], 16 * stores(i))

        @block.gpsimd
        def _(pool):
            nc.gpsimd.iota(iota_i[:], pattern=[[1, SPAN]], base=0, channel_multiplier=0).then_inc(c_iota, 1)
            nc.gpsimd.iota(part_i[:], pattern=[[1, 1]], base=0, channel_multiplier=1).then_inc(c_iota, 1)
            nc.gpsimd.memset(ident[:], 0.0).then_inc(c_id0, 1)
            pool.wait_ge(c_id0, 1)
            nc.gpsimd.affine_select(out=ident[:], in_=ident[:], compare_op=ALU.not_equal, fill=1.0, base=0,
                                    pattern=[[-1, P]], channel_multiplier=1).then_inc(c_iota, 1)
            pool.wait_ge(l_cols, 32)
            fit = fits(pool)
            for i in range(2):
                pool.wait_ge(w_kv[i], 16 * len(range(i, STAGES, 2)))
            with pool.If(fit == 1):
                for group in range(GROUPS):
                    slot = group % KV_RING
                    if group >= KV_RING:
                        pool.wait_ge(e_msg, group - KV_RING + 1)
                    for t in range(tiles_of(group)):
                        tile = group * GROUP_TILES + t
                        pool.indirect_dma_start(
                            kv[:, slot, t, :], None, kv_table,
                            bass.IndirectOffsetOnAxis(ap=src_idx[:, tile:tile + 1], axis=0)
                        ).then_inc(e_kv[slot], 16)
            with pool.Else():
                for i in range(2):
                    pool.wait_ge(w_q[i], 16 * len(range(i, STAGES, 2)))
                with pool.Fori(0, GROUPS) as group:
                    pool.wait_ge(g_free, group + 1)
                    cols = bass.ds(group * GROUP_TILES, GROUP_TILES)
                    nc.gpsimd.tensor_copy(g_src[:], src_idx[:, cols]).then_inc(g_idx, 1)
                    nc.gpsimd.tensor_copy(g_dst[:], dst_idx[:, cols]).then_inc(g_idx, 1)
                    pool.wait_ge(g_idx, group * 2 + 2)
                    pool.sem_inc(g_step, 1)
                    for t in range(GROUP_TILES):
                        pool.indirect_dma_start(
                            kv[:, 0, t, :], None, kv_table,
                            bass.IndirectOffsetOnAxis(ap=g_src[:, t:t + 1], axis=0)).then_inc(g_gather, 16)
                        pool.indirect_dma_start(
                            g_q[:, t, :], None, q_table,
                            bass.IndirectOffsetOnAxis(ap=g_dst[:, t:t + 1], axis=0)).then_inc(g_gather, 16)

        @block.scalar
        def _(act):
            act.dma_start(rows_i[:], dst_rows).then_inc(l_idx, 16)
            act.dma_start(src_idx[:], src_cols).then_inc(l_cols, 16)
            act.dma_start(dst_idx[:], dst_cols).then_inc(l_cols, 16)
            act.dma_start(x_n[:], x_rows.rearrange("(t p) d -> p t d", p=P)).then_inc(l_xn, 16)

            def statistics():
                act.wait_ge(r_chain, 6)
                act.dma_start(base_dram.rearrange("(n j) -> n j", j=2), row_min[:]).then_inc(r_store, 16)
                act.dma_start(span_dram.rearrange("(n j) -> n j", j=2), row_span[:]).then_inc(r_store, 16)
                act.dma_start(rel_rows_dram.rearrange("(n j) e -> n j e", j=2), rows_rel[:]).then_inc(r_rel, 16)
                act.wait_ge(r_store, 32)
                act.dma_start(base_all[:], base_dram.rearrange("(o n) -> o n", o=1).to_broadcast([P, GROUPS])
                              ).then_inc(r_load, 16)
                act.dma_start(span_row[:], span_dram.rearrange("(o n) -> o n", o=1)).then_inc(r_load, 16)

            for tile in range(TABLE_TILES):
                stage, t = divmod(tile, STAGE_TILES)
                if stage >= 2 and t == 0:
                    act.wait_ge(w_kv[stage % 2], 16 * (stage // 2))
                act.wait_ge(t_mm, tile + 1)
                nc.scalar.copy(kv_stage[:, stage % 2, t, :], ps_table_kv[tile % 4][:, 0:2 * DIM]).then_inc(t_kv, 1)
                if tile == STAGE_TILES:
                    statistics()
            fit = fits(act)
            with act.If(fit == 1):
                for group in range(GROUPS):
                    n = tiles_of(group)
                    act.wait_ge(e_clip, group + 1)
                    if group >= 3:
                        act.wait_ge(e_seg, group - 2)
                    nc.scalar.activation(msg[:, group % 3, 0:n, DIM:SUMS], clipped[:, group % 2, 0:n, :], ACT.Exp
                                         ).then_inc(e_exp, 1)
            with act.Else():
                with act.Fori(0, GROUPS) as group:
                    act.wait_ge(g_clip, group + 1)
                    nc.scalar.activation(msg[:, 0, :, DIM:SUMS], clipped[:, 0], ACT.Exp).then_inc(g_exp, 1)
            for step in range(n_final):
                n = min(FINAL_TILES, NODE_TILES - step * FINAL_TILES)
                act.wait_ge(f_cen, step + 1)
                nc.scalar.activation(sq[:, step % 2, 0:n, :], y[:, step % 2, 0:n, :], ACT.Square
                                     ).then_inc(f_sq, 1)
                act.wait_ge(f_var, step + 1)
                nc.scalar.activation(rstd[:, step % 2, 0:n], var[:, step % 2, 0:n], ACT.Sqrt,
                                     bias=eps_norm[:], scale=1.0 / DIM).then_inc(f_sqrt, 1)

        @block.vector
        def _(dve):
            n_chain = {}

            def link(semaphore, instruction):
                n_chain[semaphore.name] = n_chain.get(semaphore.name, 0) + 1
                instruction.then_inc(semaphore, 1)
                dve.wait_ge(semaphore, n_chain[semaphore.name])

            nc.vector.memset(x_t[DIM:DIM + 1, :], 1.0)
            nc.vector.memset(ea[DIM:DIM + 1, :, :], 1.0)
            nc.vector.memset(eps_norm[:], EPS_NORM)
            nc.vector.memset(acc_t[:], 0.0).then_inc(c_ones, 1)
            dve.wait_ge(c_iota, 3)
            nc.vector.tensor_copy(iota[:], iota_i[:])
            nc.vector.tensor_copy(part_iota[:], part_i[:]).then_inc(c_iota_f, 1)

            def statistics():
                dve.wait_ge(l_idx, 16)
                link(r_chain, nc.vector.tensor_copy(rows_f[:], rows_i[:]))
                nc.vector.tensor_reduce(row_min[:], rows_f[:], axis=AX_X, op=ALU.min).then_inc(r_chain, 1)
                nc.vector.tensor_reduce(row_max[:], rows_f[:], axis=AX_X, op=ALU.max).then_inc(r_chain, 1)
                dve.wait_ge(r_chain, 3)
                nc.vector.tensor_tensor(row_span[:], row_max[:], row_min[:], ALU.subtract).then_inc(r_chain, 1)
                for j in range(2):
                    nc.vector.tensor_scalar(rows_rel[:, j, :], rows_f[:, j, :], row_min[:, j:j + 1], None,
                                            ALU.subtract).then_inc(r_chain, 1)
                dve.wait_ge(l_cols, 32)
                nc.vector.tensor_copy(dst_f[:], dst_idx[:]).then_inc(r_cols, 1)

            def bases():
                dve.wait_ge(r_load, 32)
                nc.vector.tensor_copy(base_i[:], base_all[0:1, :]).then_inc(r_cols, 1)
                nc.vector.tensor_reduce(span_max[:], span_row[:], axis=AX_X, op=ALU.max).then_inc(r_cols, 1)
                dve.wait_ge(r_cols, 3)
                nc.vector.tensor_scalar(fits_i[:], span_max[:], float(WINDOW), None, ALU.is_lt).then_inc(r_cols, 1)
                dve.wait_ge(r_cols, 4)
                nc.vector.tensor_tensor(
                    rel_f[:].rearrange("p (n t) -> p n t", t=GROUP_TILES),
                    dst_f[:].rearrange("p (n t) -> p n t", t=GROUP_TILES),
                    base_all[:].unsqueeze(2).to_broadcast([P, GROUPS, GROUP_TILES]), ALU.subtract
                ).then_inc(r_cols, 1)
                dve.wait_ge(r_cols, 5)
                dve.sem_inc(r_ready, 1)

            for stage in range(STAGES):
                dve.wait_ge(t_mq, stage + 1)
                link(t_q, nc.vector.tensor_scalar(
                    q_full[:], ps_table_q[stage % 2][:, 0:STAGE_TILES * DIM].rearrange("p (t d) -> p t d", d=DIM),
                    float(HEAD_DIM) ** -0.5, None, ALU.mult))
                if stage >= 2:
                    dve.wait_ge(w_q[stage % 2], 16 * (stage // 2))
                part = [q_stage[:, stage % 2, :, j * DIM:(j + 1) * DIM] for j in range(3)]
                link(t_split, nc.vector.tensor_copy(part[0], q_full[:]))
                link(t_split, nc.vector.tensor_tensor(q_rest[:], q_full[:], part[0], ALU.subtract))
                link(t_split, nc.vector.tensor_copy(part[1], q_rest[:]))
                link(t_split, nc.vector.tensor_tensor(q_rest2[:], q_rest[:], part[1], ALU.subtract))
                link(t_split, nc.vector.tensor_copy(part[2], q_rest2[:]))
                if stage == 0:
                    statistics()
                if stage == 3:
                    bases()

            fit = fits(dve)

            def make_pick_t(group):
                pair, half, n = group // 2, group % 2, tiles_of(group) * P
                slot = pair % REL_RING
                dve.wait_ge(e_rel[slot], 16 * (pair // REL_RING + 1))
                if group >= 3:
                    dve.wait_ge(e_q, group - 2)
                nc.vector.tensor_scalar(pick_t[:, group % 3, 0:n], rel_bc[:, slot, half * GROUP:half * GROUP + n],
                                        part_iota[:], None, ALU.is_equal).then_inc(e_pt, 1)

            def make_pick(group):
                n = tiles_of(group)
                if group >= 3:
                    dve.wait_ge(e_seg, group - 2)
                rel = rel_f[:, group * GROUP_TILES:group * GROUP_TILES + n]
                nc.vector.tensor_tensor(pick[:, group % 3, 0:n, :],
                                        iota[:, 0:WINDOW].unsqueeze(1).to_broadcast([P, n, WINDOW]),
                                        rel.unsqueeze(2).to_broadcast([P, n, WINDOW]), ALU.is_equal
                                        ).then_inc(e_pick, 1)

            def k_times_q(group):
                n = tiles_of(group)
                slot = group % KV_RING
                fetched = sum(tiles_of(g) for g in range(slot, group + 1, KV_RING))
                dve.wait_ge(e_kv[slot], 16 * fetched)
                dve.wait_ge(e_q, group + 1)
                if group >= 2:
                    dve.wait_ge(e_kqe, group - 1)
                nc.vector.tensor_tensor(kq[:, group % 2, 0:n, :], kv[:, slot, 0:n, 0:DIM],
                                        ps_q[group % 2][:, 0:n * DIM].rearrange("p (t d) -> p t d", t=n),
                                        ALU.mult).then_inc(e_kq, 1)

            def times_e(group):
                n = tiles_of(group)
                dve.wait_ge(e_kq, group + 1)
                dve.wait_ge(e_e, group + 1)
                nc.vector.tensor_tensor(kqe[:, group % 2, 0:n, :], kq[:, group % 2, 0:n, :],
                                        ps_e[group % 2][:, 0:n * DIM].rearrange("p (t d) -> p t d", t=n),
                                        ALU.mult).then_inc(e_kqe, 1)

            def sum_heads(group):
                n = tiles_of(group)
                dve.wait_ge(e_kqe, group + 1)
                nc.vector.tensor_reduce(score[:, group % 2, 0:n, :],
                                        kqe[:, group % 2, 0:n, :].rearrange("p t (h d) -> p t h d", h=HEADS),
                                        axis=AX_X, op=ALU.add).then_inc(e_sum, 1)

            def clip(group):
                n = tiles_of(group)
                dve.wait_ge(e_sum, group + 1)
                if group >= 2:
                    dve.wait_ge(e_exp, group - 1)
                nc.vector.tensor_scalar(clipped[:, group % 2, 0:n, :], score[:, group % 2, 0:n, :],
                                        CLIP, -CLIP, ALU.min, ALU.max).then_inc(e_clip, 1)

            def weigh_v(group):
                n = tiles_of(group)
                dve.wait_ge(e_exp, group + 1)
                m = msg[:, group % 3, 0:n, :]
                nc.vector.tensor_tensor(
                    m[:, :, 0:DIM].rearrange("p t (h d) -> p t h d", h=HEADS),
                    kv[:, group % KV_RING, 0:n, DIM:2 * DIM].rearrange("p t (h d) -> p t h d", h=HEADS),
                    m[:, :, DIM:SUMS].unsqueeze(3).to_broadcast([P, n, HEADS, HEAD_DIM]), ALU.mult
                ).then_inc(e_msg, 1)

            def accumulate(group):
                base = base_of(dve, group)
                dve.wait_ge(e_seg, group + 1)
                if group:
                    dve.wait_ge(e_acc, group)
                window = acc_t[:, bass.ds(base, WINDOW)]
                nc.vector.tensor_tensor(window, window, ps_seg[group % 2][0:SUMS, 0:WINDOW], ALU.add
                                        ).then_inc(e_acc, 1)

            with dve.If(fit == 1):
                for group in range(2):
                    make_pick_t(group)
                make_pick(0)
                for group in range(GROUPS + 2):
                    if group + 2 < GROUPS:
                        make_pick_t(group + 2)
                    if group < GROUPS:
                        k_times_q(group)
                    if 2 <= group:
                        accumulate(group - 2)
                    if group < GROUPS:
                        times_e(group)
                    if group + 1 < GROUPS:
                        make_pick(group + 1)
                    if group < GROUPS:
                        sum_heads(group)
                    if 1 <= group <= GROUPS:
                        weigh_v(group - 1)
                    if group < GROUPS:
                        clip(group)
                dve.wait_ge(e_acc, GROUPS)
            with dve.Else():
                dve.sem_inc(g_free, 1)
                per_group = 7 + SPANS
                with dve.Fori(0, GROUPS) as group:
                    done = [0]

                    def then(instruction):
                        done[0] += 1
                        instruction.then_inc(g_chain, 1)
                        dve.wait_ge(g_chain, group * per_group + done[0])

                    cols = bass.ds(group * GROUP_TILES, GROUP_TILES)
                    then(nc.vector.tensor_copy(g_dst_f[:], dst_f[:, cols]))
                    dve.wait_ge(g_gather, group * (32 * GROUP_TILES) + 32 * GROUP_TILES)
                    part = [g_q[:, :, j * DIM:(j + 1) * DIM] for j in range(3)]
                    then(nc.vector.tensor_tensor(kq[:, 0], part[0], part[1], ALU.add))
                    then(nc.vector.tensor_tensor(kqe[:, 0], kq[:, 0], part[2], ALU.add))
                    then(nc.vector.tensor_tensor(kq[:, 0], kqe[:, 0], kv[:, 0, :, 0:DIM], ALU.mult))
                    dve.wait_ge(g_e, group + 1)
                    then(nc.vector.tensor_tensor(kqe[:, 0], kq[:, 0], ps_e[0][:, 0:GROUP_TILES * DIM].rearrange(
                        "p (t d) -> p t d", t=GROUP_TILES), ALU.mult))
                    then(nc.vector.tensor_reduce(score[:, 0], kqe[:, 0].rearrange("p t (h d) -> p t h d", h=HEADS),
                                                 axis=AX_X, op=ALU.add))
                    nc.vector.tensor_scalar(clipped[:, 0], score[:, 0], CLIP, -CLIP, ALU.min, ALU.max
                                            ).then_inc(g_clip, 1)
                    dve.wait_ge(g_exp, group + 1)
                    m = msg[:, 0]
                    then(nc.vector.tensor_tensor(
                        m[:, :, 0:DIM].rearrange("p t (h d) -> p t h d", h=HEADS),
                        kv[:, 0, :, DIM:2 * DIM].rearrange("p t (h d) -> p t h d", h=HEADS),
                        m[:, :, DIM:SUMS].unsqueeze(3).to_broadcast([P, GROUP_TILES, HEADS, HEAD_DIM]), ALU.mult))
                    for span in range(SPANS):
                        for t in range(GROUP_TILES):
                            last = nc.vector.tensor_scalar(g_pick[:, t, :], iota[:], float(span * SPAN),
                                                           g_dst_f[:, t:t + 1], ALU.add, ALU.is_equal)
                        last.then_inc(g_pk, 1)
                        dve.wait_ge(g_seg, group * SPANS + (span + 1))
                        nodes = acc_t[:, span * SPAN:(span + 1) * SPAN]
                        then(nc.vector.tensor_tensor(nodes, nodes, ps_seg[0][0:SUMS, :], ALU.add))
                    dve.sem_inc(g_free, 1)
            dve.sem_inc(f_acc, 1)

            dve.wait_ge(l_xn, 16)
            for step in range(n_final):
                first, s = step * FINAL_TILES, step % 2
                n = min(FINAL_TILES, NODE_TILES - first)
                dve.wait_ge(f_tr, step + 1)
                sums = ps_fin[s][:, 0:n * SUMS].rearrange("p (t c) -> p t c", t=n)
                heads = lambda a: a.rearrange("p t (h d) -> p t h d", h=HEADS)
                link(f_chain, nc.vector.tensor_scalar(z_eps[:, s, 0:n, :], sums[:, :, DIM:SUMS], EPS_Z, None, ALU.add))
                link(f_chain, nc.vector.reciprocal(z_inv[:, s, 0:n, :], z_eps[:, s, 0:n, :]))
                nc.vector.tensor_tensor(heads(h[:, s, 0:n, :]), heads(sums[:, :, 0:DIM]),
                                        z_inv[:, s, 0:n, :].unsqueeze(3).to_broadcast([P, n, HEADS, HEAD_DIM]),
                                        ALU.mult).then_inc(f_div, 1)
                dve.wait_ge(f_div, step + 1)
                link(f_chain, nc.vector.tensor_tensor(h[:, s, 0:n, :], h[:, s, 0:n, :], x_n[:, first:first + n, :],
                                                      ALU.add))
                link(f_chain, nc.vector.tensor_reduce(mean[:, s, 0:n], h[:, s, 0:n, :], axis=AX_X, op=ALU.add))
                link(f_chain, nc.vector.tensor_scalar(mean[:, s, 0:n], mean[:, s, 0:n], 1.0 / DIM, None, ALU.mult))
                if step >= 2:
                    dve.wait_ge(f_out[s], 16 * stores(s, step))
                wide = lambda a: a.unsqueeze(2).to_broadcast([P, n, DIM])
                nc.vector.tensor_tensor(y[:, s, 0:n, :], h[:, s, 0:n, :], wide(mean[:, s, 0:n]), ALU.subtract
                                        ).then_inc(f_cen, 1)
                dve.wait_ge(f_sq, step + 1)
                nc.vector.tensor_reduce(var[:, s, 0:n], sq[:, s, 0:n, :], axis=AX_X, op=ALU.add).then_inc(f_var, 1)
                dve.wait_ge(f_sqrt, step + 1)
                link(f_chain, nc.vector.reciprocal(rstd[:, s, 0:n], rstd[:, s, 0:n]))
                nc.vector.tensor_tensor(y[:, s, 0:n, :], y[:, s, 0:n, :], wide(rstd[:, s, 0:n]), ALU.mult
                                        ).then_inc(f_y, 1)

        @block.tensor
        def _(pe):
            pe.wait_ge(c_ones, 1)
            pe.wait_ge(l_w, 16 * 8)
            for tile in range(TABLE_TILES):
                if tile % STAGE_TILES == 0:
                    pe.wait_ge(l_x[tile // STAGE_TILES], 16)
                if tile >= 4:
                    pe.wait_ge(t_kv, tile - 3)
                nodes = x_t[:, tile * P:(tile + 1) * P]
                nc.tensor.matmul(ps_table_kv[tile % 4][:, 0:2 * DIM], nodes, w_cat[:, 0:2 * DIM],
                                 start=True, stop=True).then_inc(t_mm, 1)
                stage, t = divmod(tile, STAGE_TILES)
                if t == 0 and stage >= 2:
                    pe.wait_ge(t_q, stage - 1)
                last = nc.tensor.matmul(ps_table_q[stage % 2][:, t * DIM:(t + 1) * DIM], nodes,
                                        w_cat[:, 2 * DIM:3 * DIM], start=True, stop=True)
                if t == STAGE_TILES - 1:
                    last.then_inc(t_mq, 1)
            pe.wait_ge(t_kv, TABLE_TILES)
            pe.wait_ge(t_q, STAGES)
            fit = fits(pe)

            def edge_features(group):
                pair, half = group // 2, group % 2
                slot = pair % EA_RING
                pe.wait_ge(e_ea[slot], 16 * (pair // EA_RING + 1))
                if group >= 2:
                    pe.wait_ge(e_kqe, group - 1)
                for t in range(tiles_of(group)):
                    at = half * GROUP + t * P
                    last = nc.tensor.matmul(ps_e[group % 2][:, t * DIM:(t + 1) * DIM], ea[:, slot, at:at + P],
                                            w_e[:], start=True, stop=True)
                last.then_inc(e_e, 1)

            def edge_queries(group):
                slot = group % QWIN_RING
                pe.wait_ge(e_qwin[slot], 16 * (group // QWIN_RING + 1))
                pe.wait_ge(e_pt, group + 1)
                if group >= 2:
                    pe.wait_ge(e_kq, group - 1)
                for t in range(tiles_of(group)):
                    for part in range(3):
                        last = nc.tensor.matmul(ps_q[group % 2][:, t * DIM:(t + 1) * DIM],
                                                pick_t[:, group % 3, t * P:(t + 1) * P],
                                                q_win[:, slot, part * DIM:(part + 1) * DIM],
                                                start=(part == 0), stop=(part == 2))
                last.then_inc(e_q, 1)

            def segment_sums(group):
                n = tiles_of(group)
                pe.wait_ge(e_pick, group + 1)
                pe.wait_ge(e_msg, group + 1)
                if group >= 2:
                    pe.wait_ge(e_acc, group - 1)
                for t in range(n):
                    last = nc.tensor.matmul(ps_seg[group % 2][0:SUMS, 0:WINDOW], msg[:, group % 3, t, :],
                                            pick[:, group % 3, t, :], start=(t == 0), stop=(t == n - 1))
                last.then_inc(e_seg, 1)

            with pe.If(fit == 1):
                edge_features(0)
                edge_queries(0)
                for group in range(GROUPS + 1):
                    if group + 1 < GROUPS:
                        edge_features(group + 1)
                        edge_queries(group + 1)
                    if group >= 1:
                        segment_sums(group - 1)
            with pe.Else():
                with pe.Fori(0, GROUPS) as group:
                    pe.wait_ge(g_ea, group * 16 + 16)
                    for t in range(GROUP_TILES):
                        last = nc.tensor.matmul(ps_e[0][:, t * DIM:(t + 1) * DIM], ea[:, 0, t * P:(t + 1) * P],
                                                w_e[:], start=True, stop=True)
                    last.then_inc(g_e, 1)
                    for span in range(SPANS):
                        pe.wait_ge(g_pk, group * SPANS + (span + 1))
                        for t in range(GROUP_TILES):
                            last = nc.tensor.matmul(ps_seg[0][0:SUMS, :], msg[:, 0, t, :], g_pick[:, t, :],
                                                    start=(t == 0), stop=(t == GROUP_TILES - 1))
                        last.then_inc(g_seg, 1)
            pe.wait_ge(f_acc, 1)
            for step in range(n_final):
                first, s = step * FINAL_TILES, step % 2
                n = min(FINAL_TILES, NODE_TILES - first)
                if step >= 2:
                    pe.wait_ge(f_div, step - 1)
                for t in range(n):
                    nodes = slice((first + t) * P, (first + t + 1) * P)
                    last = nc.tensor.transpose(ps_fin[s][:, t * SUMS:(t + 1) * SUMS], acc_t[:, nodes],
                                               ident[0:SUMS, 0:SUMS])
                last.then_inc(f_tr, 1)


def kernel(x, src, dst, edge_attr_96, L0_gnn_Wq, L0_gnn_bq, L0_gnn_Wk, L0_gnn_bk, L0_gnn_We, L0_gnn_be,
           L0_gnn_Wv, L0_gnn_bv):
    import concourse.bacc as bacc
    from concourse.bass_utils import run_bass_kernel_spmd

    x, src, dst, edge_attr = (np.asarray(a) for a in (x, src, dst, edge_attr_96))
    x_rows = np.zeros((TABLE_ROWS, DIM), x.dtype)
    x_rows[:N_NODES] = x
    ea_t = np.zeros((DIM, EDGES_PADDED), edge_attr.dtype)
    ea_t[:, :N_EDGES] = edge_attr.T
    src_padded = np.zeros(EDGES_PADDED, src.dtype)
    src_padded[:N_EDGES] = src
    dst_padded = np.full(EDGES_PADDED, N_NODES, dst.dtype)
    dst_padded[:N_EDGES] = dst

    arrays = {
        "x_t_in": np.ascontiguousarray(x_rows.T),
        "x_rows_in": x_rows,
        "src_cols_in": np.ascontiguousarray(src_padded.reshape(-1, P).T).view(np.uint32),
        "dst_cols_in": np.ascontiguousarray(dst_padded.reshape(-1, P).T).view(np.uint32),
        "dst_rows_in": dst_padded.reshape(PAIRS, 2, GROUP),
        "ea_t_in": ea_t,
    }
    for name, a in (("q", L0_gnn_Wq), ("k", L0_gnn_Wk), ("v", L0_gnn_Wv), ("e", L0_gnn_We)):
        arrays[f"w_{name}_in"] = np.ascontiguousarray(a)
    for name, a in (("q", L0_gnn_bq), ("k", L0_gnn_bk), ("v", L0_gnn_bv), ("e", L0_gnn_be)):
        arrays[f"b_{name}_in"] = np.ascontiguousarray(a).reshape(1, DIM)

    nc = bacc.Bacc("TRN2", target_bir_lowering=False, num_devices=1)
    ap = {n: nc.dram_tensor(n, a.shape, mybir.dt.from_np(a.dtype), kind="ExternalInput").ap()
          for n, a in arrays.items()}
    out = nc.dram_tensor("out", [N_NODES, DIM], F32, kind="ExternalOutput").ap()
    build(nc, ap["x_t_in"], ap["x_rows_in"], ap["src_cols_in"], ap["dst_cols_in"], ap["dst_rows_in"],
          ap["ea_t_in"], {n: ap[f"w_{n}_in"] for n in "qkve"}, {n: ap[f"b_{n}_in"] for n in "qkve"}, out)
    r = run_bass_kernel_spmd(nc, [arrays], core_ids=[0])
    return r.results[0]["out"]
```

```python
from contextlib import ExitStack

import numpy as np

import concourse.bass as bass
from concourse import mybir

F32 = mybir.dt.float32
BF16 = mybir.dt.bfloat16
I32 = mybir.dt.int32
U32 = mybir.dt.uint32
ALU = mybir.AluOpType
ACT = mybir.ActivationFunctionType
AX_X = mybir.AxisListType.X

P = 128
N_NODES, N_EDGES = 6250, 100000
HEADS, HEAD_DIM = 8, 12
DIM = HEADS * HEAD_DIM
SUMS = DIM + HEADS
EPS_Z, EPS_NORM, CLIP = 1e-6, 1e-5, 5.0

GROUP_TILES = 4
GROUP = GROUP_TILES * P
GROUPS = -(-N_EDGES // GROUP)
TILES = -(-N_EDGES // P)
EDGES_PADDED = GROUPS * GROUP
PAIRS = GROUPS // 2
WINDOW = 96

NODE_TILES = -(-N_NODES // P)
TABLE_TILES = NODE_TILES + 1
TABLE_ROWS = TABLE_TILES * P
KV_STAGE = 10
KV_STAGES = TABLE_TILES // KV_STAGE
Q_STAGE = 5
Q_STAGES = TABLE_TILES // Q_STAGE
SPAN = 512
SPANS = -(-(N_NODES + 1) // SPAN)
ACC_NODES = SPANS * SPAN
FINAL_TILES = 4

FINAL_RING = 4
KV_RING, EA_RING, REL_RING, QWIN_RING = 8, 3, 3, 4


def tiles_of(group):
    return min(GROUP_TILES, TILES - group * GROUP_TILES)


def build(nc, xT, x_rows, src_cols, dst_cols, dst_rows, eaT, weights, biases, ones, out):
    assert GROUPS % 2 == 0 and TABLE_TILES % KV_STAGE == 0 and KV_STAGE % 2 == 0 and TABLE_TILES % Q_STAGE == 0
    assert N_NODES + WINDOW <= ACC_NODES and N_NODES + P <= TABLE_ROWS + 1

    kv_table = nc.dram_tensor("kv_table", [TABLE_ROWS, 2 * DIM], F32).ap()
    q_table = nc.dram_tensor("q_table", [TABLE_ROWS, 3 * DIM], BF16).ap()
    rel_rows_dram = nc.dram_tensor("rel_rows_dram", [GROUPS, GROUP], BF16).ap()
    base_dram = nc.dram_tensor("base_dram", [GROUPS], F32).ap()
    span_dram = nc.dram_tensor("span_dram", [GROUPS], F32).ap()

    with ExitStack() as ctx:
        def sb(name, shape, dt):
            return ctx.enter_context(nc.sbuf_tensor(name, shape, dt))

        def psum(name, shape):
            return ctx.enter_context(nc.psum_tensor(name, shape, F32))

        def sem(name):
            return ctx.enter_context(nc.semaphore(name))

        iota_i = sb("iota_i", [P, SPAN], I32)
        iota = sb("iota", [P, SPAN], F32)
        part_i = sb("part_i", [P, 1], I32)
        part_iota = sb("part_iota", [P, 1], F32)
        ident = sb("ident", [P, P], F32)
        eps_norm = sb("eps_norm", [P, 1], F32)

        x_both = sb("x_both", [P, TABLE_ROWS], F32)
        x_t = x_both[0:DIM + 1, :]
        x_n = x_both[:, 0:TABLE_TILES * DIM].rearrange("p (t d) -> p t d", d=DIM)
        w_all = sb("w_all", [DIM + 1, 4 * DIM], F32)
        w_kv, w_q, w_e = w_all[:, 0:2 * DIM], w_all[:, 2 * DIM:3 * DIM], w_all[:, 3 * DIM:4 * DIM]
        kv_stage = sb("kv_stage", [P, 2, KV_STAGE, 2 * DIM], F32)
        q_stage = sb("q_stage", [P, 2, Q_STAGE, 3 * DIM], BF16)
        q_full = sb("q_full", [P, 2, Q_STAGE, DIM], F32)
        q_rest = sb("q_rest", [P, Q_STAGE, DIM], F32)

        src_idx = sb("src_idx", [P, GROUPS * GROUP_TILES], U32)
        dst_idx = sb("dst_idx", [P, GROUPS * GROUP_TILES], U32)
        dst_f = sb("dst_f", [P, GROUPS * GROUP_TILES], F32)
        rel_f = sb("rel_f", [P, GROUPS * GROUP_TILES], F32)
        base_all = sb("base_all", [P, GROUPS], F32)
        rows_i = sb("rows_i", [PAIRS, 2, GROUP], I32)
        rows_f = sb("rows_f", [PAIRS, 2, GROUP], F32)
        rows_rel = sb("rows_rel", [PAIRS, 2, GROUP], BF16)
        row_min = sb("row_min", [PAIRS, 2], F32)
        row_max = sb("row_max", [PAIRS, 2], F32)
        row_span = sb("row_span", [PAIRS, 2], F32)
        span_row = sb("span_row", [1, GROUPS], F32)
        span_max = sb("span_max", [1, 1], F32)
        base_i = sb("base_i", [1, GROUPS], I32)
        fits_i = sb("fits_i", [1, 1], I32)

        kv = sb("kv", [P, KV_RING, GROUP_TILES, 2 * DIM], F32)
        ea = sb("ea", [DIM + 1, EA_RING, 2 * GROUP], F32)
        rel_bc = sb("rel_bc", [P, REL_RING, 2 * GROUP], BF16)
        q_win = sb("q_win", [P, QWIN_RING, 3 * DIM], BF16)
        pick_t = sb("pick_t", [P, 3, GROUP], BF16)
        pick = sb("pick", [P, 3, GROUP_TILES, WINDOW], F32)
        kq = sb("kq", [P, 2, GROUP_TILES, DIM], F32)
        kqe = sb("kqe", [P, 2, GROUP_TILES, DIM], F32)
        score = sb("score", [P, 2, GROUP_TILES, HEADS], F32)
        clipped = sb("clipped", [P, 2, GROUP_TILES, HEADS], F32)
        msg = sb("msg", [P, 3, GROUP_TILES, SUMS], F32)
        acc_t = sb("acc_t", [SUMS, ACC_NODES], F32)

        g_src = sb("g_src", [P, GROUP_TILES], U32)
        g_dst = sb("g_dst", [P, GROUP_TILES], U32)
        g_dst_f = sb("g_dst_f", [P, GROUP_TILES], F32)
        g_q = sb("g_q", [P, GROUP_TILES, 3 * DIM], BF16)
        g_pick = sb("g_pick", [P, GROUP_TILES, SPAN], F32)

        z_inv = sb("z_inv", [P, FINAL_RING, FINAL_TILES, HEADS], F32)
        z_eps = sb("z_eps", [P, FINAL_RING, FINAL_TILES, HEADS], F32)
        h = sb("h", [P, FINAL_RING, FINAL_TILES, DIM], F32)
        hx = sb("hx", [P, FINAL_RING, FINAL_TILES, DIM], F32)
        total = sb("total", [P, FINAL_RING, FINAL_TILES], F32)
        neg_mean = sb("neg_mean", [P, FINAL_RING, FINAL_TILES], F32)
        var = sb("var", [P, FINAL_RING, FINAL_TILES], F32)
        std = sb("std", [P, FINAL_RING, FINAL_TILES], F32)
        rstd = sb("rstd", [P, FINAL_RING, FINAL_TILES], F32)
        y = sb("y", [P, FINAL_RING, FINAL_TILES, DIM], F32)

        ps_e = [psum(f"ps_e{i}", [P, 512]) for i in range(2)]
        ps_q = [psum(f"ps_q{i}", [P, 512]) for i in range(2)]
        ps_seg = [psum(f"ps_seg{i}", [P, 512]) for i in range(2)]
        ps_table_kv, ps_table_q = ps_e + ps_seg, ps_q
        ps_fin = ps_e + ps_seg

        l_x = [sem(f"l_x{i}") for i in range(KV_STAGES)]
        l_w = sem("l_w")
        l_rows = sem("l_rows")
        l_cols = sem("l_cols")
        l_xn = sem("l_xn")
        c_xones = sem("c_xones")
        c_iota = sem("c_iota")
        c_id0 = sem("c_id0")
        c_ident = sem("c_ident")
        c_ea = sem("c_ea")
        c_iota_f = sem("c_iota_f")
        c_eps = sem("c_eps")
        c_acc = sem("c_acc")
        t_mm = sem("t_mm")
        t_mq = sem("t_mq")
        t_kv = sem("t_kv")
        t_q = sem("t_q")
        t_split = sem("t_split")
        d_kv = [sem(f"d_kv{i}") for i in range(2)]
        d_q = [sem(f"d_q{i}") for i in range(2)]
        r_chain = sem("r_chain")
        r_store = sem("r_store")
        r_rel = sem("r_rel")
        r_load = sem("r_load")
        r_ready = sem("r_ready")
        r_cols = sem("r_cols")
        e_kv = [sem(f"e_kv{i}") for i in range(KV_RING)]
        e_ea = [sem(f"e_ea{i}") for i in range(EA_RING)]
        e_rel = [sem(f"e_rel{i}") for i in range(REL_RING)]
        e_qwin = [sem(f"e_qwin{i}") for i in range(QWIN_RING)]
        e_pt = sem("e_pt")
        e_pick = sem("e_pick")
        e_e = sem("e_e")
        e_q = sem("e_q")
        e_kq = sem("e_kq")
        e_kqe = sem("e_kqe")
        e_sum = sem("e_sum")
        e_clip = sem("e_clip")
        e_exp = sem("e_exp")
        e_msg = sem("e_msg")
        e_seg = sem("e_seg")
        e_acc = sem("e_acc")
        g_free = sem("g_free")
        g_idx = sem("g_idx")
        g_step = sem("g_step")
        g_gather = sem("g_gather")
        g_ea = sem("g_ea")
        g_e = sem("g_e")
        g_clip = sem("g_clip")
        g_exp = sem("g_exp")
        g_pk = sem("g_pk")
        g_seg = sem("g_seg")
        g_chain = sem("g_chain")
        f_acc = sem("f_acc")
        f_tr = sem("f_tr")
        f_div = sem("f_div")
        f_z = sem("f_z")
        f_hx = sem("f_hx")
        f_mean = sem("f_mean")
        f_std = sem("f_std")
        f_var = sem("f_var")
        f_rstd = sem("f_rstd")
        f_y = sem("f_y")
        f_out = [sem(f"f_out{i}") for i in range(FINAL_RING)]

        n_final = -(-NODE_TILES // FINAL_TILES)
        kv_store = kv_table.rearrange("(t p) d -> p t d", p=P)
        q_store = q_table.rearrange("(t p) d -> p t d", p=P)

        def stores(slot, before=None):
            n = 0
            for step in range(slot, n_final if before is None else before, FINAL_RING):
                first = step * FINAL_TILES
                tiles = min(FINAL_TILES, NODE_TILES - first)
                whole = tiles if (first + tiles) * P <= N_NODES else tiles - 1
                n += (whole > 0) + (whole < tiles)
            return n

        def fits(eng):
            eng.wait_ge(r_ready, 1)
            return eng.value_load(fits_i[0:1, 0:1], min_val=0, max_val=1)

        def base_of(eng, group):
            return eng.value_load(base_i[0:1, group:group + 1], min_val=0, max_val=N_NODES)

        block = ctx.enter_context(nc.Block())

        @block.sync
        def _(sp):
            for i in range(KV_STAGES):
                cols = slice(i * KV_STAGE * P, (i + 1) * KV_STAGE * P)
                sp.dma_start(x_t[0:DIM, cols], xT[:, cols]).then_inc(l_x[i], 16)
                if i == 0:
                    sp.dma_start(w_all[0:DIM, :], weights).then_inc(l_w, 16)
                    sp.dma_start(w_all[DIM:DIM + 1, :], biases).then_inc(l_w, 16)
            for i in range(KV_STAGES):
                sp.wait_ge(t_kv, (i + 1) * KV_STAGE // 2)
                sp.dma_start(kv_store[:, i * KV_STAGE:(i + 1) * KV_STAGE, :], kv_stage[:, i % 2]
                             ).then_inc(d_kv[i % 2], 16)
            for i in range(Q_STAGES):
                sp.wait_ge(t_split, 4 * (i + 1))
                sp.dma_start(q_store[:, i * Q_STAGE:(i + 1) * Q_STAGE, :], q_stage[:, i % 2]
                             ).then_inc(d_q[i % 2], 16)
            sp.wait_ge(r_rel, 16)
            fit = fits(sp)
            with sp.If(fit == 1):
                for i in range(2):
                    sp.wait_ge(d_q[i], 16 * len(range(i, Q_STAGES, 2)))
                sp.wait_ge(c_ea, 16)
                rel_pairs = rel_rows_dram.rearrange("(n j) e -> n (j e)", j=2)
                for pair in range(PAIRS):
                    slot, use = pair % EA_RING, pair // EA_RING
                    if use:
                        sp.wait_ge(e_e, 2 * (pair - EA_RING) + 2)
                    sp.dma_start(ea[0:DIM, slot, :], eaT[:, pair * 2 * GROUP:(pair + 1) * 2 * GROUP]
                                 ).then_inc(e_ea[slot], 16)
                    slot, use = pair % REL_RING, pair // REL_RING
                    if use:
                        sp.wait_ge(e_pt, 2 * (pair - REL_RING) + 2)
                    sp.dma_start(rel_bc[:, slot, :], rel_pairs[pair:pair + 1, :].to_broadcast([P, 2 * GROUP])
                                 ).then_inc(e_rel[slot], 16)
                    for group in (2 * pair, 2 * pair + 1):
                        base = base_of(sp, group)
                        slot, use = group % QWIN_RING, group // QWIN_RING
                        if use:
                            sp.wait_ge(e_q, group - QWIN_RING + 1)
                        sp.dma_start(q_win[:, slot, :], q_table[bass.ds(base, P), :]).then_inc(e_qwin[slot], 16)
            with sp.Else():
                sp.wait_ge(c_ea, 16)
                with sp.Fori(0, GROUPS) as group:
                    sp.wait_ge(g_free, group + 1)
                    sp.dma_start(ea[0:DIM, 0, 0:GROUP], eaT[:, bass.ds(group * GROUP, GROUP)]).then_inc(g_ea, 16)
            for step in range(n_final):
                first = step * FINAL_TILES
                n = min(FINAL_TILES, NODE_TILES - first)
                sp.wait_ge(f_y, step + 1)
                whole = n if (first + n) * P <= N_NODES else n - 1
                if whole:
                    sp.dma_start(out[first * P:(first + whole) * P, :].rearrange("(t p) d -> p t d", p=P),
                                 y[:, step % FINAL_RING, 0:whole, :]).then_inc(f_out[step % FINAL_RING], 16)
                if whole < n:
                    left = N_NODES - (first + whole) * P
                    sp.dma_start(out[(first + whole) * P:N_NODES, :],
                                 y[0:left, step % FINAL_RING, whole, :]).then_inc(f_out[step % FINAL_RING], 16)
            for i in range(FINAL_RING):
                sp.wait_ge(f_out[i], 16 * stores(i))

        @block.gpsimd
        def _(pool):
            pool.dma_start(dst_idx[:], dst_cols).then_inc(l_cols, 16)
            pool.dma_start(src_idx[:], src_cols).then_inc(l_cols, 16)
            nc.gpsimd.iota(iota_i[:], pattern=[[1, SPAN]], base=0, channel_multiplier=0).then_inc(c_iota, 1)
            nc.gpsimd.iota(part_i[:], pattern=[[1, 1]], base=0, channel_multiplier=1).then_inc(c_iota, 1)
            pool.wait_ge(r_chain, 6)
            pool.dma_start(base_dram.rearrange("(n j) -> n j", j=2), row_min[:]).then_inc(r_store, 16)
            pool.dma_start(span_dram.rearrange("(n j) -> n j", j=2), row_span[:]).then_inc(r_store, 16)
            pool.dma_start(rel_rows_dram.rearrange("(n j) e -> n j e", j=2), rows_rel[:]).then_inc(r_rel, 16)
            pool.wait_ge(r_store, 32)
            pool.dma_start(base_all[:], base_dram.rearrange("(o n) -> o n", o=1).to_broadcast([P, GROUPS])
                           ).then_inc(r_load, 16)
            pool.dma_start(span_row[:], span_dram.rearrange("(o n) -> o n", o=1)).then_inc(r_load, 16)
            nc.gpsimd.memset(acc_t[:], 0.0).then_inc(c_acc, 1)
            nc.gpsimd.memset(ident[:], 0.0).then_inc(c_id0, 1)
            pool.wait_ge(c_id0, 1)
            nc.gpsimd.affine_select(out=ident[:], in_=ident[:], compare_op=ALU.not_equal, fill=1.0, base=0,
                                    pattern=[[-1, P]], channel_multiplier=1).then_inc(c_ident, 1)
            pool.wait_ge(l_cols, 32)
            fit = fits(pool)
            for i in range(2):
                pool.wait_ge(d_kv[i], 16 * len(range(i, KV_STAGES, 2)))
            with pool.If(fit == 1):
                for group in range(GROUPS):
                    slot = group % KV_RING
                    if group >= KV_RING:
                        pool.wait_ge(e_msg, group - KV_RING + 1)
                    for t in range(tiles_of(group)):
                        tile = group * GROUP_TILES + t
                        pool.indirect_dma_start(
                            kv[:, slot, t, :], None, kv_table,
                            bass.IndirectOffsetOnAxis(ap=src_idx[:, tile:tile + 1], axis=0)
                        ).then_inc(e_kv[slot], 16)
            with pool.Else():
                for i in range(2):
                    pool.wait_ge(d_q[i], 16 * len(range(i, Q_STAGES, 2)))
                with pool.Fori(0, GROUPS) as group:
                    pool.wait_ge(g_free, group + 1)
                    cols = bass.ds(group * GROUP_TILES, GROUP_TILES)
                    nc.gpsimd.tensor_copy(g_src[:], src_idx[:, cols]).then_inc(g_idx, 1)
                    nc.gpsimd.tensor_copy(g_dst[:], dst_idx[:, cols]).then_inc(g_idx, 1)
                    pool.wait_ge(g_idx, group * 2 + 2)
                    pool.sem_inc(g_step, 1)
                    for t in range(GROUP_TILES):
                        pool.indirect_dma_start(
                            kv[:, 0, t, :], None, kv_table,
                            bass.IndirectOffsetOnAxis(ap=g_src[:, t:t + 1], axis=0)).then_inc(g_gather, 16)
                        pool.indirect_dma_start(
                            g_q[:, t, :], None, q_table,
                            bass.IndirectOffsetOnAxis(ap=g_dst[:, t:t + 1], axis=0)).then_inc(g_gather, 16)

            pool.wait_ge(l_xn, 16)
            for step in range(n_final):
                first, s = step * FINAL_TILES, step % FINAL_RING
                n = min(FINAL_TILES, NODE_TILES - first)
                pool.wait_ge(f_div, step + 1)
                if step >= FINAL_RING:
                    pool.wait_ge(f_y, step - FINAL_RING + 1)
                nc.gpsimd.tensor_tensor(hx[:, s, 0:n, :], h[:, s, 0:n, :], x_n[:, first:first + n, :], ALU.add
                                        ).then_inc(f_hx, 1)

        @block.scalar
        def _(act):
            act.dma_start(rows_i[:], dst_rows).then_inc(l_rows, 16)
            act.dma_start(x_t[DIM:DIM + 1, :], ones[0:1, :]).then_inc(c_xones, 16)
            act.dma_start(ea[DIM:DIM + 1, :, :], ones[0:1, 0:EA_RING * 2 * GROUP]).then_inc(c_ea, 16)
            for pair in range(TABLE_TILES // 2):
                stage, t = divmod(2 * pair, KV_STAGE)
                if stage >= 2 and t == 0:
                    act.wait_ge(d_kv[stage % 2], 16 * (stage // 2))
                act.wait_ge(t_mm, pair + 1)
                nc.scalar.copy(kv_stage[:, stage % 2, t:t + 2, :],
                               ps_table_kv[pair % 4][:, 0:4 * DIM].rearrange("p (t d) -> p t d", t=2)
                               ).then_inc(t_kv, 1)
            for stage in range(Q_STAGES):
                act.wait_ge(t_mq, stage + 1)
                if stage >= 2:
                    act.wait_ge(t_split, 4 * (stage - 1))
                nc.scalar.mul(q_full[:, stage % 2],
                              ps_table_q[stage % 2][:, 0:Q_STAGE * DIM].rearrange("p (t d) -> p t d", d=DIM),
                              float(HEAD_DIM) ** -0.5).then_inc(t_q, 1)
            act.dma_start(x_n, x_rows.rearrange("(t p) d -> p t d", p=P)).then_inc(l_xn, 16)
            fit = fits(act)
            with act.If(fit == 1):
                for group in range(GROUPS):
                    n = tiles_of(group)
                    act.wait_ge(e_clip, group + 1)
                    if group >= 3:
                        act.wait_ge(e_seg, group - 2)
                    nc.scalar.activation(msg[:, group % 3, 0:n, DIM:SUMS], clipped[:, group % 2, 0:n, :], ACT.Exp
                                         ).then_inc(e_exp, 1)
            with act.Else():
                with act.Fori(0, GROUPS) as group:
                    act.wait_ge(g_clip, group + 1)
                    nc.scalar.activation(msg[:, 0, :, DIM:SUMS], clipped[:, 0], ACT.Exp).then_inc(g_exp, 1)
            act.wait_ge(c_eps, 1)
            for step in range(n_final + 1):
                if step < n_final:
                    s, n = step % FINAL_RING, min(FINAL_TILES, NODE_TILES - step * FINAL_TILES)
                    act.wait_ge(f_mean, 2 * step + 2)
                    if step >= FINAL_RING:
                        act.wait_ge(f_out[s], 16 * stores(s, step))
                    for t in range(n):
                        nc.scalar.activation(y[:, s, t, :], hx[:, s, t, :], ACT.Square,
                                             bias=neg_mean[:, s, t:t + 1],
                                             accum_out=var[:, s, t:t + 1]).then_inc(f_var, 1)
                if step:
                    s, n = (step - 1) % FINAL_RING, min(FINAL_TILES, NODE_TILES - (step - 1) * FINAL_TILES)
                    act.wait_ge(f_var, (step - 1) * FINAL_TILES + n)
                    nc.scalar.activation(std[:, s, 0:n], var[:, s, 0:n], ACT.Sqrt,
                                         bias=eps_norm[:], scale=1.0 / DIM).then_inc(f_std, 1)

        @block.vector
        def _(dve):
            n_chain = {}

            def link(semaphore, instruction):
                n_chain[semaphore.name] = n_chain.get(semaphore.name, 0) + 1
                instruction.then_inc(semaphore, 1)
                dve.wait_ge(semaphore, n_chain[semaphore.name])

            nc.vector.memset(eps_norm[:], EPS_NORM).then_inc(c_eps, 1)

            def statistics():
                dve.wait_ge(l_rows, 16)
                link(r_chain, nc.vector.tensor_copy(rows_f[:], rows_i[:]))
                nc.vector.tensor_reduce(row_min[:], rows_f[:], axis=AX_X, op=ALU.min).then_inc(r_chain, 1)
                nc.vector.tensor_reduce(row_max[:], rows_f[:], axis=AX_X, op=ALU.max).then_inc(r_chain, 1)
                dve.wait_ge(r_chain, 3)
                nc.vector.tensor_tensor(row_span[:], row_max[:], row_min[:], ALU.subtract).then_inc(r_chain, 1)
                for j in range(2):
                    nc.vector.tensor_scalar(rows_rel[:, j, :], rows_f[:, j, :], row_min[:, j:j + 1], None,
                                            ALU.subtract).then_inc(r_chain, 1)
                dve.wait_ge(l_cols, 32)
                nc.vector.tensor_copy(dst_f[:], dst_idx[:]).then_inc(r_cols, 1)

            def bases():
                dve.wait_ge(r_load, 32)
                nc.vector.tensor_copy(base_i[:], base_all[0:1, :]).then_inc(r_cols, 1)
                nc.vector.tensor_reduce(span_max[:], span_row[:], axis=AX_X, op=ALU.max).then_inc(r_cols, 1)
                dve.wait_ge(r_cols, 3)
                nc.vector.tensor_scalar(fits_i[:], span_max[:], float(WINDOW), None, ALU.is_lt).then_inc(r_cols, 1)
                dve.wait_ge(r_cols, 4)
                nc.vector.tensor_tensor(
                    rel_f[:].rearrange("p (n t) -> p n t", t=GROUP_TILES),
                    dst_f[:].rearrange("p (n t) -> p n t", t=GROUP_TILES),
                    base_all[:].unsqueeze(2).to_broadcast([P, GROUPS, GROUP_TILES]), ALU.subtract
                ).then_inc(r_cols, 1)
                dve.wait_ge(r_cols, 5)
                dve.sem_inc(r_ready, 1)

            statistics()
            dve.wait_ge(c_iota, 2)
            nc.vector.tensor_copy(iota[:], iota_i[:]).then_inc(c_iota_f, 1)
            nc.vector.tensor_copy(part_iota[:], part_i[:]).then_inc(c_iota_f, 1)
            bases()
            for stage in range(Q_STAGES):
                if stage >= 2:
                    dve.wait_ge(d_q[stage % 2], 16 * (stage // 2))
                dve.wait_ge(t_q, stage + 1)
                part = [q_stage[:, stage % 2, :, j * DIM:(j + 1) * DIM] for j in range(3)]
                full = q_full[:, stage % 2]
                link(t_split, nc.vector.tensor_copy(part[0], full))
                link(t_split, nc.vector.tensor_tensor(q_rest[:], full, part[0], ALU.subtract))
                link(t_split, nc.vector.tensor_copy(part[1], q_rest[:]))
                link(t_split, nc.vector.tensor_tensor(part[2], q_rest[:], part[1], ALU.subtract))
            dve.wait_ge(c_iota_f, 2)
            dve.wait_ge(c_acc, 1)
            fit = fits(dve)

            def make_pick_t(group):
                pair, half, n = group // 2, group % 2, tiles_of(group) * P
                slot = pair % REL_RING
                dve.wait_ge(e_rel[slot], 16 * (pair // REL_RING + 1))
                if group >= 3:
                    dve.wait_ge(e_q, group - 2)
                nc.vector.tensor_scalar(pick_t[:, group % 3, 0:n], rel_bc[:, slot, half * GROUP:half * GROUP + n],
                                        part_iota[:], None, ALU.is_equal).then_inc(e_pt, 1)

            def make_pick(group):
                n = tiles_of(group)
                if group >= 3:
                    dve.wait_ge(e_seg, group - 2)
                rel = rel_f[:, group * GROUP_TILES:group * GROUP_TILES + n]
                nc.vector.tensor_tensor(pick[:, group % 3, 0:n, :],
                                        iota[:, 0:WINDOW].unsqueeze(1).to_broadcast([P, n, WINDOW]),
                                        rel.unsqueeze(2).to_broadcast([P, n, WINDOW]), ALU.is_equal
                                        ).then_inc(e_pick, 1)

            def k_times_q(group):
                n = tiles_of(group)
                slot = group % KV_RING
                fetched = sum(tiles_of(g) for g in range(slot, group + 1, KV_RING))
                dve.wait_ge(e_kv[slot], 16 * fetched)
                dve.wait_ge(e_q, group + 1)
                if group >= 2:
                    dve.wait_ge(e_kqe, group - 1)
                nc.vector.tensor_tensor(kq[:, group % 2, 0:n, :], kv[:, slot, 0:n, 0:DIM],
                                        ps_q[group % 2][:, 0:n * DIM].rearrange("p (t d) -> p t d", t=n),
                                        ALU.mult).then_inc(e_kq, 1)

            def times_e(group):
                n = tiles_of(group)
                dve.wait_ge(e_kq, group + 1)
                dve.wait_ge(e_e, group + 1)
                nc.vector.tensor_tensor(kqe[:, group % 2, 0:n, :], kq[:, group % 2, 0:n, :],
                                        ps_e[group % 2][:, 0:n * DIM].rearrange("p (t d) -> p t d", t=n),
                                        ALU.mult).then_inc(e_kqe, 1)

            def sum_heads(group):
                n = tiles_of(group)
                dve.wait_ge(e_kqe, group + 1)
                nc.vector.tensor_reduce(score[:, group % 2, 0:n, :],
                                        kqe[:, group % 2, 0:n, :].rearrange("p t (h d) -> p t h d", h=HEADS),
                                        axis=AX_X, op=ALU.add).then_inc(e_sum, 1)

            def clip(group):
                n = tiles_of(group)
                dve.wait_ge(e_sum, group + 1)
                if group >= 2:
                    dve.wait_ge(e_exp, group - 1)
                nc.vector.tensor_scalar(clipped[:, group % 2, 0:n, :], score[:, group % 2, 0:n, :],
                                        CLIP, -CLIP, ALU.min, ALU.max).then_inc(e_clip, 1)

            def weigh_v(group):
                n = tiles_of(group)
                dve.wait_ge(e_exp, group + 1)
                m = msg[:, group % 3, 0:n, :]
                nc.vector.tensor_tensor(
                    m[:, :, 0:DIM].rearrange("p t (h d) -> p t h d", h=HEADS),
                    kv[:, group % KV_RING, 0:n, DIM:2 * DIM].rearrange("p t (h d) -> p t h d", h=HEADS),
                    m[:, :, DIM:SUMS].unsqueeze(3).to_broadcast([P, n, HEADS, HEAD_DIM]), ALU.mult
                ).then_inc(e_msg, 1)

            def accumulate(group):
                base = base_of(dve, group)
                dve.wait_ge(e_seg, group + 1)
                if group:
                    dve.wait_ge(e_acc, group)
                window = acc_t[:, bass.ds(base, WINDOW)]
                nc.vector.tensor_tensor(window, window, ps_seg[group % 2][0:SUMS, 0:WINDOW], ALU.add
                                        ).then_inc(e_acc, 1)

            with dve.If(fit == 1):
                for group in range(2):
                    make_pick_t(group)
                make_pick(0)
                for group in range(GROUPS + 2):
                    if group + 2 < GROUPS:
                        make_pick_t(group + 2)
                    if group < GROUPS:
                        k_times_q(group)
                    if 2 <= group:
                        accumulate(group - 2)
                    if group < GROUPS:
                        times_e(group)
                    if group + 1 < GROUPS:
                        make_pick(group + 1)
                    if group < GROUPS:
                        sum_heads(group)
                    if 1 <= group <= GROUPS:
                        weigh_v(group - 1)
                    if group < GROUPS:
                        clip(group)
                dve.wait_ge(e_acc, GROUPS)
            with dve.Else():
                dve.sem_inc(g_free, 1)
                per_group = 7 + SPANS
                with dve.Fori(0, GROUPS) as group:
                    done = [0]

                    def then(instruction):
                        done[0] += 1
                        instruction.then_inc(g_chain, 1)
                        dve.wait_ge(g_chain, group * per_group + done[0])

                    cols = bass.ds(group * GROUP_TILES, GROUP_TILES)
                    then(nc.vector.tensor_copy(g_dst_f[:], dst_f[:, cols]))
                    dve.wait_ge(g_gather, group * (32 * GROUP_TILES) + 32 * GROUP_TILES)
                    part = [g_q[:, :, j * DIM:(j + 1) * DIM] for j in range(3)]
                    then(nc.vector.tensor_tensor(kq[:, 0], part[0], part[1], ALU.add))
                    then(nc.vector.tensor_tensor(kqe[:, 0], kq[:, 0], part[2], ALU.add))
                    then(nc.vector.tensor_tensor(kq[:, 0], kqe[:, 0], kv[:, 0, :, 0:DIM], ALU.mult))
                    dve.wait_ge(g_e, group + 1)
                    then(nc.vector.tensor_tensor(kqe[:, 0], kq[:, 0], ps_e[0][:, 0:GROUP_TILES * DIM].rearrange(
                        "p (t d) -> p t d", t=GROUP_TILES), ALU.mult))
                    then(nc.vector.tensor_reduce(score[:, 0], kqe[:, 0].rearrange("p t (h d) -> p t h d", h=HEADS),
                                                 axis=AX_X, op=ALU.add))
                    nc.vector.tensor_scalar(clipped[:, 0], score[:, 0], CLIP, -CLIP, ALU.min, ALU.max
                                            ).then_inc(g_clip, 1)
                    dve.wait_ge(g_exp, group + 1)
                    m = msg[:, 0]
                    then(nc.vector.tensor_tensor(
                        m[:, :, 0:DIM].rearrange("p t (h d) -> p t h d", h=HEADS),
                        kv[:, 0, :, DIM:2 * DIM].rearrange("p t (h d) -> p t h d", h=HEADS),
                        m[:, :, DIM:SUMS].unsqueeze(3).to_broadcast([P, GROUP_TILES, HEADS, HEAD_DIM]), ALU.mult))
                    for span in range(SPANS):
                        for t in range(GROUP_TILES):
                            last = nc.vector.tensor_scalar(g_pick[:, t, :], iota[:], float(span * SPAN),
                                                           g_dst_f[:, t:t + 1], ALU.add, ALU.is_equal)
                        last.then_inc(g_pk, 1)
                        dve.wait_ge(g_seg, group * SPANS + (span + 1))
                        nodes = acc_t[:, span * SPAN:(span + 1) * SPAN]
                        then(nc.vector.tensor_tensor(nodes, nodes, ps_seg[0][0:SUMS, :], ALU.add))
                    dve.sem_inc(g_free, 1)
            dve.sem_inc(f_acc, 1)

            def divide(step):
                first, s = step * FINAL_TILES, step % FINAL_RING
                n = min(FINAL_TILES, NODE_TILES - first)
                heads = lambda a: a.rearrange("p t (h d) -> p t h d", h=HEADS)
                sums = ps_fin[step % len(ps_fin)][:, 0:n * SUMS].rearrange("p (t c) -> p t c", t=n)
                dve.wait_ge(f_tr, step + 1)
                nc.vector.tensor_scalar(z_eps[:, s, 0:n, :], sums[:, :, DIM:SUMS], EPS_Z, None, ALU.add
                                        ).then_inc(f_z, 1)
                dve.wait_ge(f_z, 2 * step + 1)
                nc.vector.reciprocal(z_inv[:, s, 0:n, :], z_eps[:, s, 0:n, :]).then_inc(f_z, 1)
                if step >= FINAL_RING:
                    dve.wait_ge(f_hx, step - FINAL_RING + 1)
                dve.wait_ge(f_z, 2 * step + 2)
                nc.vector.tensor_tensor(heads(h[:, s, 0:n, :]), heads(sums[:, :, 0:DIM]),
                                        z_inv[:, s, 0:n, :].unsqueeze(3).to_broadcast([P, n, HEADS, HEAD_DIM]),
                                        ALU.mult).then_inc(f_div, 1)

            def means(step):
                s, n = step % FINAL_RING, min(FINAL_TILES, NODE_TILES - step * FINAL_TILES)
                dve.wait_ge(f_hx, step + 1)
                nc.vector.tensor_reduce(total[:, s, 0:n], hx[:, s, 0:n, :], axis=AX_X, op=ALU.add
                                        ).then_inc(f_mean, 1)
                dve.wait_ge(f_mean, 2 * step + 1)
                nc.vector.tensor_scalar(neg_mean[:, s, 0:n], total[:, s, 0:n], -1.0 / DIM, None, ALU.mult
                                        ).then_inc(f_mean, 1)

            def normalise(step):
                s, n = step % FINAL_RING, min(FINAL_TILES, NODE_TILES - step * FINAL_TILES)
                dve.wait_ge(f_std, step + 1)
                nc.vector.reciprocal(rstd[:, s, 0:n], std[:, s, 0:n]).then_inc(f_rstd, 1)
                dve.wait_ge(f_rstd, step + 1)
                for t in range(n):
                    last = nc.vector.tensor_scalar(y[:, s, t, :], hx[:, s, t, :], neg_mean[:, s, t:t + 1],
                                                   rstd[:, s, t:t + 1], ALU.add, ALU.mult)
                last.then_inc(f_y, 1)

            for step in range(n_final + 2):
                if step < n_final:
                    divide(step)
                if 1 <= step <= n_final:
                    means(step - 1)
                if step >= 2:
                    normalise(step - 2)

        @block.tensor
        def _(pe):
            pe.wait_ge(c_xones, 16)
            pe.wait_ge(l_w, 32)
            for tile in range(TABLE_TILES):
                pair, half = divmod(tile, 2)
                if tile % KV_STAGE == 0:
                    pe.wait_ge(l_x[tile // KV_STAGE], 16)
                if half == 0 and pair >= 4:
                    pe.wait_ge(t_kv, pair - 3)
                last = nc.tensor.matmul(ps_table_kv[pair % 4][:, half * 2 * DIM:(half + 1) * 2 * DIM],
                                        x_t[:, tile * P:(tile + 1) * P], w_kv, start=True, stop=True)
                if half == 1:
                    last.then_inc(t_mm, 1)
            for tile in range(TABLE_TILES):
                stage, t = divmod(tile, Q_STAGE)
                if t == 0 and stage >= 2:
                    pe.wait_ge(t_q, stage - 1)
                last = nc.tensor.matmul(ps_table_q[stage % 2][:, t * DIM:(t + 1) * DIM],
                                        x_t[:, tile * P:(tile + 1) * P], w_q, start=True, stop=True)
                if t == Q_STAGE - 1:
                    last.then_inc(t_mq, 1)
            pe.wait_ge(t_kv, TABLE_TILES // 2)
            pe.wait_ge(t_q, Q_STAGES)
            pe.wait_ge(c_ea, 16)
            fit = fits(pe)

            def edge_features(group):
                pair, half = group // 2, group % 2
                slot = pair % EA_RING
                pe.wait_ge(e_ea[slot], 16 * (pair // EA_RING + 1))
                if group >= 2:
                    pe.wait_ge(e_kqe, group - 1)
                for t in range(tiles_of(group)):
                    at = half * GROUP + t * P
                    last = nc.tensor.matmul(ps_e[group % 2][:, t * DIM:(t + 1) * DIM], ea[:, slot, at:at + P],
                                            w_e, start=True, stop=True)
                last.then_inc(e_e, 1)

            def edge_queries(group):
                slot = group % QWIN_RING
                pe.wait_ge(e_qwin[slot], 16 * (group // QWIN_RING + 1))
                pe.wait_ge(e_pt, group + 1)
                if group >= 2:
                    pe.wait_ge(e_kq, group - 1)
                for t in range(tiles_of(group)):
                    for part in range(3):
                        last = nc.tensor.matmul(ps_q[group % 2][:, t * DIM:(t + 1) * DIM],
                                                pick_t[:, group % 3, t * P:(t + 1) * P],
                                                q_win[:, slot, part * DIM:(part + 1) * DIM],
                                                start=(part == 0), stop=(part == 2))
                last.then_inc(e_q, 1)

            def segment_sums(group):
                n = tiles_of(group)
                pe.wait_ge(e_pick, group + 1)
                pe.wait_ge(e_msg, group + 1)
                if group >= 2:
                    pe.wait_ge(e_acc, group - 1)
                for t in range(n):
                    last = nc.tensor.matmul(ps_seg[group % 2][0:SUMS, 0:WINDOW], msg[:, group % 3, t, :],
                                            pick[:, group % 3, t, :], start=(t == 0), stop=(t == n - 1))
                last.then_inc(e_seg, 1)

            with pe.If(fit == 1):
                edge_features(0)
                edge_queries(0)
                for group in range(GROUPS + 1):
                    if group + 1 < GROUPS:
                        edge_features(group + 1)
                        edge_queries(group + 1)
                    if group >= 1:
                        segment_sums(group - 1)
            with pe.Else():
                with pe.Fori(0, GROUPS) as group:
                    pe.wait_ge(g_ea, group * 16 + 16)
                    for t in range(GROUP_TILES):
                        last = nc.tensor.matmul(ps_e[0][:, t * DIM:(t + 1) * DIM], ea[:, 0, t * P:(t + 1) * P],
                                                w_e, start=True, stop=True)
                    last.then_inc(g_e, 1)
                    for span in range(SPANS):
                        pe.wait_ge(g_pk, group * SPANS + (span + 1))
                        for t in range(GROUP_TILES):
                            last = nc.tensor.matmul(ps_seg[0][0:SUMS, :], msg[:, 0, t, :], g_pick[:, t, :],
                                                    start=(t == 0), stop=(t == GROUP_TILES - 1))
                        last.then_inc(g_seg, 1)
            pe.wait_ge(f_acc, 1)
            pe.wait_ge(c_ident, 1)
            for step in range(n_final):
                first, bank = step * FINAL_TILES, ps_fin[step % len(ps_fin)]
                n = min(FINAL_TILES, NODE_TILES - first)
                if step >= len(ps_fin):
                    pe.wait_ge(f_div, step - len(ps_fin) + 1)
                for t in range(n):
                    nodes = slice((first + t) * P, (first + t + 1) * P)
                    last = nc.tensor.transpose(bank[:, t * SUMS:(t + 1) * SUMS], acc_t[:, nodes],
                                               ident[0:SUMS, 0:SUMS])
                last.then_inc(f_tr, 1)


def kernel(x, src, dst, edge_attr_96, L0_gnn_Wq, L0_gnn_bq, L0_gnn_Wk, L0_gnn_bk, L0_gnn_We, L0_gnn_be,
           L0_gnn_Wv, L0_gnn_bv):
    import concourse.bacc as bacc
    from concourse.bass_utils import run_bass_kernel_spmd

    x, src, dst, edge_attr = (np.asarray(a) for a in (x, src, dst, edge_attr_96))
    x_rows = np.zeros((TABLE_ROWS, DIM), x.dtype)
    x_rows[:N_NODES] = x
    ea_t = np.zeros((DIM, EDGES_PADDED), edge_attr.dtype)
    ea_t[:, :N_EDGES] = edge_attr.T
    src_padded = np.zeros(EDGES_PADDED, src.dtype)
    src_padded[:N_EDGES] = src
    dst_padded = np.full(EDGES_PADDED, N_NODES, dst.dtype)
    dst_padded[:N_EDGES] = dst

    arrays = {
        "x_t_in": np.ascontiguousarray(x_rows.T),
        "x_rows_in": x_rows,
        "src_cols_in": np.ascontiguousarray(src_padded.reshape(-1, P).T).view(np.uint32),
        "dst_cols_in": np.ascontiguousarray(dst_padded.reshape(-1, P).T).view(np.uint32),
        "dst_rows_in": dst_padded.reshape(PAIRS, 2, GROUP),
        "ea_t_in": ea_t,
    }
    arrays["weights_in"] = np.concatenate([L0_gnn_Wk, L0_gnn_Wv, L0_gnn_Wq, L0_gnn_We], axis=1)
    arrays["biases_in"] = np.concatenate([L0_gnn_bk, L0_gnn_bv, L0_gnn_bq, L0_gnn_be]).reshape(1, 4 * DIM)

    arrays["ones_in"] = np.ones((1, TABLE_ROWS), np.float32)

    nc = bacc.Bacc("TRN2", target_bir_lowering=False, num_devices=1)
    ap = {n: nc.dram_tensor(n, a.shape, mybir.dt.from_np(a.dtype), kind="ExternalInput").ap()
          for n, a in arrays.items()}
    out = nc.dram_tensor("out", [N_NODES, DIM], F32, kind="ExternalOutput").ap()
    build(nc, ap["x_t_in"], ap["x_rows_in"], ap["src_cols_in"], ap["dst_cols_in"], ap["dst_rows_in"],
          ap["ea_t_in"], ap["weights_in"], ap["biases_in"], ap["ones_in"], out)
    r = run_bass_kernel_spmd(nc, [arrays], core_ids=[0])
    return r.results[0]["out"]
```

```python
import math
from contextlib import ExitStack

import numpy as np

import concourse.bass as bass
from concourse import mybir

F32 = mybir.dt.float32
BF16 = mybir.dt.bfloat16
I32 = mybir.dt.int32
U32 = mybir.dt.uint32
ALU = mybir.AluOpType
ACT = mybir.ActivationFunctionType
AX_X = mybir.AxisListType.X

P = 128
N_NODES, N_EDGES = 6250, 100000
HEADS, HEAD_DIM = 8, 12
DIM = HEADS * HEAD_DIM
SUMS = DIM + HEADS
EPS_Z, EPS_NORM, CLIP = 1e-6, 1e-5, 5.0

GROUP_TILES = 4
GROUP = GROUP_TILES * P
GROUPS = -(-N_EDGES // GROUP)
TILES = -(-N_EDGES // P)
EDGES_PADDED = GROUPS * GROUP
PAIRS = GROUPS // 2
WINDOW = 80
EARLY = 8

NODE_TILES = -(-N_NODES // P)
TABLE_TILES = NODE_TILES + 1
TABLE_ROWS = TABLE_TILES * P
KV_STAGE = 10
KV_STAGES = TABLE_TILES // KV_STAGE
Q_STAGE = 5
Q_STAGES = TABLE_TILES // Q_STAGE
Q_BUFFERS = 4
PARTS = 3
X_PARTS = 10
X_PARTS_FROM, X_PARTS_EVERY = 2 * EARLY, 4
SPAN = 512
SPANS = -(-(N_NODES + 1) // SPAN)
ACC_NODES = SPANS * SPAN

FINAL_TILES = 4
STEP_NODES = FINAL_TILES * P
STEPS = -(-NODE_TILES // FINAL_TILES)
FINAL_RING = 3
KV_RING, EA_RING, REL_RING, QWIN_RING, PICK_RING, MSG_RING = 17, 3, 3, 8, 4, 3

GENERAL, WINDOWED, STREAMED = 0, 1, 2
FINISHED_AFTER = [math.ceil(GROUPS * math.sqrt((step + 1) * STEP_NODES / N_NODES)) + 1 for step in range(STEPS - 1)]
LAG_TRANSPOSE, LAG_DIVIDE, LAG_SQUARE, LAG_NORMALISE = 3, 4, 5, 6
STREAMED_STEPS = sum(after + LAG_NORMALISE < GROUPS for after in FINISHED_AFTER)


def tiles_of(group):
    return min(GROUP_TILES, TILES - group * GROUP_TILES)


def steps_at(group, lag, streamed):
    return [s for s in range(STREAMED_STEPS) if FINISHED_AFTER[s] + lag == group] if streamed else []


def steps_left(streamed):
    return range(STREAMED_STEPS if streamed else 0, STEPS)


def tiles_in(step):
    return min(FINAL_TILES, NODE_TILES - step * FINAL_TILES)


def stores_of(step):
    first, n = step * FINAL_TILES, tiles_in(step)
    whole = min(n, N_NODES // P - first)
    return [(0, whole, P)] * (whole > 0) + [(whole, 1, N_NODES % P)] * (whole < n)


def stores_before(step):
    return sum(len(stores_of(s)) for s in range(step % FINAL_RING, step, FINAL_RING))


def build(nc, xT, x_rows, src_cols, dst_cols, dst_rows, eaT, weights, biases, ones, out):
    assert GROUPS % 2 == 0 and TABLE_TILES % KV_STAGE == 0 and KV_STAGE % 2 == 0 and TABLE_TILES % Q_STAGE == 0
    assert N_NODES + WINDOW <= ACC_NODES and N_NODES + P <= TABLE_ROWS + 1
    assert X_PARTS_FROM + X_PARTS * X_PARTS_EVERY < FINISHED_AFTER[0]
    assert EA_RING == REL_RING and EARLY + 2 <= Q_STAGES and WINDOW <= P
    assert EARLY < KV_RING and tiles_of(EARLY) == GROUP_TILES

    kv_table = nc.dram_tensor("kv_table", [TABLE_ROWS, 2 * DIM], F32).ap()
    q_table = nc.dram_tensor("q_table", [TABLE_ROWS, PARTS * DIM], BF16).ap()
    rel_rows_dram = nc.dram_tensor("rel_rows_dram", [GROUPS, GROUP], BF16).ap()
    base_dram = nc.dram_tensor("base_dram", [GROUPS], F32).ap()
    span_dram = nc.dram_tensor("span_dram", [GROUPS], F32).ap()

    with ExitStack() as ctx:
        def sb(name, shape, dt):
            return ctx.enter_context(nc.sbuf_tensor(name, shape, dt))

        def psum(name):
            return ctx.enter_context(nc.psum_tensor(name, [P, 512], F32))

        def sem(name):
            return ctx.enter_context(nc.semaphore(name))

        iota_i = sb("iota_i", [P, SPAN], I32)
        iota = sb("iota", [P, SPAN], F32)
        part_i = sb("part_i", [P, 1], I32)
        neg_part = sb("neg_part", [P, 1], F32)
        ident = sb("ident", [P, P], F32)
        eps_norm = sb("eps_norm", [P, 1], F32)
        sqrt_eps = sb("sqrt_eps", [P, 1], F32)

        x_both = sb("x_both", [P, TABLE_ROWS], F32)
        x_t = x_both[0:DIM + 1, :]
        x_n = x_both[:, 0:TABLE_TILES * DIM].rearrange("p (t d) -> p t d", d=DIM)
        w_all = sb("w_all", [DIM + 1, 4 * DIM], F32)
        w_kv, w_q, w_e = w_all[:, 0:2 * DIM], w_all[:, 2 * DIM:3 * DIM], w_all[:, 3 * DIM:4 * DIM]
        q_both = sb("q_both", [P, 4, Q_STAGE, DIM], F32)
        q_full, q_rest = q_both[:, 0:2], q_both[:, 2:4]
        q_parts = sb("q_parts", [P, Q_BUFFERS, Q_STAGE, PARTS, DIM], BF16)
        early_t = sb("early_t", [DIM + 1, 2, GROUP], F32)

        kv_stage = sb("kv_stage", [P, 2, KV_STAGE, 2 * DIM], F32)
        stage_row = kv_stage[:].rearrange("p a t d -> p (a t d)")
        results = stage_row[:, 0:2 * FINAL_RING * FINAL_TILES * DIM].rearrange(
            "p (b s t d) -> p b s t d", b=2, s=FINAL_RING, t=FINAL_TILES)
        msg = stage_row[:, 2 * FINAL_RING * FINAL_TILES * DIM:][:, 0:MSG_RING * GROUP_TILES * SUMS].rearrange(
            "p (s t c) -> p s t c", s=MSG_RING, t=GROUP_TILES)
        h, y = results[:, 0], results[:, 1]

        src_idx = sb("src_idx", [P, GROUPS * GROUP_TILES], U32)
        dst_idx = sb("dst_idx", [P, GROUPS * GROUP_TILES], U32)
        dst_f = sb("dst_f", [P, GROUPS * GROUP_TILES], F32)
        rel_f = sb("rel_f", [P, GROUPS * GROUP_TILES], F32)
        base_all = sb("base_all", [P, GROUPS], F32)
        rows_i = sb("rows_i", [PAIRS, 2, GROUP], I32)
        rows_rel = sb("rows_rel", [PAIRS, 2, GROUP], BF16)
        row_min = sb("row_min", [PAIRS, 2], F32)
        row_max = sb("row_max", [PAIRS, 2], F32)
        row_span = sb("row_span", [PAIRS, 2], F32)
        span_row = sb("span_row", [1, GROUPS], F32)
        span_max = sb("span_max", [1, 1], F32)
        least_after = sb("least_after", [1, STREAMED_STEPS], F32)
        step_end = sb("step_end", [1, STREAMED_STEPS], F32)
        room = sb("room", [1, STREAMED_STEPS], F32)
        room_min = sb("room_min", [1, 1], F32)
        fits = sb("fits", [1, 1], F32)
        streams = sb("streams", [1, 1], F32)
        base_i = sb("base_i", [1, GROUPS], I32)
        path_i = sb("path_i", [1, 1], I32)

        kv = sb("kv", [P, KV_RING, GROUP_TILES, 2 * DIM], F32)
        ea = sb("ea", [DIM + 1, EA_RING, 2 * GROUP], F32)
        rel_bc = sb("rel_bc", [P, REL_RING, 2 * GROUP], BF16)
        q_win = sb("q_win", [P, QWIN_RING, PARTS * DIM], BF16)
        distance = sb("distance", [P, 2, GROUP], BF16)
        pick_t = sb("pick_t", [P, 3, GROUP], BF16)
        pick = q_both[:].rearrange("p b t d -> p (b t d)")[:, 0:PICK_RING * GROUP_TILES * WINDOW].rearrange(
            "p (s t n) -> p s t n", s=PICK_RING, t=GROUP_TILES)
        kq = sb("kq", [P, 2, GROUP_TILES, DIM], F32)
        kqe = sb("kqe", [P, 2, GROUP_TILES, DIM], F32)
        score = sb("score", [P, 2, GROUP_TILES, HEADS], F32)
        clipped = sb("clipped", [P, 2, GROUP_TILES, HEADS], F32)
        acc_t = sb("acc_t", [SUMS, ACC_NODES], F32)
        rows_f = acc_t[0:PAIRS, 0:2 * GROUP].rearrange("p (j e) -> p j e", j=2)

        g_src = sb("g_src", [P, GROUP_TILES], U32)
        g_dst = sb("g_dst", [P, GROUP_TILES], U32)
        g_dst_f = sb("g_dst_f", [P, GROUP_TILES], F32)
        g_q = sb("g_q", [P, GROUP_TILES, PARTS * DIM], BF16)
        g_pick = kv[:, EARLY:].rearrange("p s t d -> p (s t d)")[:, 0:GROUP_TILES * SPAN].rearrange(
            "p (t n) -> p t n", t=GROUP_TILES)

        z_inv = sb("z_inv", [P, FINAL_RING, FINAL_TILES, HEADS], F32)
        z_eps = sb("z_eps", [P, FINAL_RING, FINAL_TILES, HEADS], F32)
        total = sb("total", [P, FINAL_RING, FINAL_TILES], F32)
        neg_mean = sb("neg_mean", [P, FINAL_RING, FINAL_TILES], F32)
        var = sb("var", [P, FINAL_RING, FINAL_TILES], F32)
        std = sb("std", [P, FINAL_RING, FINAL_TILES], F32)
        rstd = sb("rstd", [P, FINAL_RING, FINAL_TILES], F32)

        ps_e = [psum(f"ps_e{i}") for i in range(2)]
        ps_q = [psum(f"ps_q{i}") for i in range(2)]
        ps_seg = [psum(f"ps_seg{i}") for i in range(2)]
        ps_node = [psum(f"ps_node{i}") for i in range(2)]
        ps_table_kv, ps_table_q, ps_early_t = ps_e + ps_seg, ps_q, ps_node

        l_x = [sem(f"l_x{i}") for i in range(KV_STAGES)]
        l_w = sem("l_w")
        l_src_early = sem("l_src_early")
        l_src = sem("l_src")
        l_rows = sem("l_rows")
        l_dst = sem("l_dst")
        l_xn = sem("l_xn")
        c_xones = sem("c_xones")
        c_ones = sem("c_ones")
        c_iota = sem("c_iota")
        c_id0 = sem("c_id0")
        c_ident = sem("c_ident")
        c_float = sem("c_float")
        c_acc = sem("c_acc")
        t_mm = sem("t_mm")
        t_mq = sem("t_mq")
        t_kv = sem("t_kv")
        t_q = sem("t_q")
        t_rest = sem("t_rest")
        d_kv = [sem(f"d_kv{i}") for i in range(2)]
        d_q = [sem(f"d_q{i}") for i in range(Q_BUFFERS)]
        x_tr = sem("x_tr")
        x_copy = sem("x_copy")
        x_mm = sem("x_mm")
        x_kv = sem("x_kv")
        r_chain = sem("r_chain")
        r_store = sem("r_store")
        r_rel = sem("r_rel")
        r_load = sem("r_load")
        r_cols = sem("r_cols")
        r_ready = sem("r_ready")
        e_kv = [sem(f"e_kv{i}") for i in range(KV_RING)]
        e_ea = [sem(f"e_ea{i}") for i in range(EA_RING)]
        e_rel = [sem(f"e_rel{i}") for i in range(REL_RING)]
        e_qwin = [sem(f"e_qwin{i}") for i in range(QWIN_RING)]
        e_dist = sem("e_dist")
        e_pt = sem("e_pt")
        e_pick = sem("e_pick")
        e_e = sem("e_e")
        e_q = sem("e_q")
        e_kq = sem("e_kq")
        e_kqe = sem("e_kqe")
        e_sum = sem("e_sum")
        e_clip = sem("e_clip")
        e_exp = sem("e_exp")
        e_msg = sem("e_msg")
        e_seg = sem("e_seg")
        e_acc = sem("e_acc")
        g_free = sem("g_free")
        g_idx = sem("g_idx")
        g_step = sem("g_step")
        g_gather = sem("g_gather")
        g_ea = sem("g_ea")
        g_e = sem("g_e")
        g_clip = sem("g_clip")
        g_exp = sem("g_exp")
        g_pk = sem("g_pk")
        g_seg = sem("g_seg")
        g_chain = sem("g_chain")
        g_acc = sem("g_acc")
        f_tr = sem("f_tr")
        f_z = sem("f_z")
        f_div = sem("f_div")
        f_hx = sem("f_hx")
        f_mean = sem("f_mean")
        f_var = sem("f_var")
        f_std = sem("f_std")
        f_rstd = sem("f_rstd")
        f_y = sem("f_y")
        f_out = [sem(f"f_out{i}") for i in range(FINAL_RING)]

        early_cols = EARLY * GROUP_TILES
        kv_store = kv_table.rearrange("(t p) d -> p t d", p=P)
        q_store = q_table.rearrange("(t p) d -> p t d", p=P)

        def path_of(eng):
            eng.wait_ge(r_ready, 1)
            return eng.value_load(path_i[0:1, 0:1], min_val=GENERAL, max_val=STREAMED)

        def base_of(eng, group):
            return eng.value_load(base_i[0:1, group:group + 1], min_val=0, max_val=N_NODES)

        def by_path(eng, path, windowed, general):
            with eng.If(path == STREAMED):
                windowed(True)
            with eng.Else():
                with eng.If(path == WINDOWED):
                    windowed(False)
                with eng.Else():
                    general()

        block = ctx.enter_context(nc.Block())

        @block.sync
        def _(sp):
            sp.dma_start(src_idx[:, 0:early_cols], src_cols[:, 0:early_cols]).then_inc(l_src_early, 16)
            sp.dma_start(w_all[0:DIM, :], weights).then_inc(l_w, 16)
            for i in range(KV_STAGES):
                cols = slice(i * KV_STAGE * P, (i + 1) * KV_STAGE * P)
                sp.dma_start(x_t[0:DIM, cols], xT[:, cols]).then_inc(l_x[i], 16)
                if i == 0:
                    sp.dma_start(w_all[DIM:DIM + 1, :], biases).then_inc(l_w, 16)
                    sp.dma_start(src_idx[:, early_cols:], src_cols[:, early_cols:]).then_inc(l_src, 16)
            sp.wait_ge(r_chain, 6)
            sp.dma_start(base_dram.rearrange("(n j) -> n j", j=2), row_min[:]).then_inc(r_store, 16)
            sp.dma_start(span_dram.rearrange("(n j) -> n j", j=2), row_span[:]).then_inc(r_store, 16)
            sp.dma_start(rel_rows_dram.rearrange("(n j) e -> n j e", j=2), rows_rel[:]).then_inc(r_rel, 16)
            for i in range(KV_STAGES):
                sp.wait_ge(t_kv, (i + 1) * KV_STAGE // 2)
                sp.dma_start(kv_store[:, i * KV_STAGE:(i + 1) * KV_STAGE, :], kv_stage[:, i % 2]
                             ).then_inc(d_kv[i % 2], 16)
                if i == 0:
                    sp.wait_ge(r_store, 32)
                    sp.dma_start(base_all[:], base_dram.rearrange("(o n) -> o n", o=1).to_broadcast([P, GROUPS])
                                 ).then_inc(r_load, 16)
                    sp.dma_start(span_row[:], span_dram.rearrange("(o n) -> o n", o=1)).then_inc(r_load, 16)
            rel_pairs = rel_rows_dram.rearrange("(n j) e -> n (j e)", j=2)

            def load_pair(pair):
                slot = pair % EA_RING
                if pair >= EA_RING:
                    sp.wait_ge(e_e, 2 * (pair - EA_RING) + 2)
                sp.dma_start(ea[0:DIM, slot, :], eaT[:, pair * 2 * GROUP:(pair + 1) * 2 * GROUP]
                             ).then_inc(e_ea[slot], 16)
                slot = pair % REL_RING
                if pair >= REL_RING:
                    sp.wait_ge(e_dist, 2 * (pair - REL_RING) + 2)
                sp.dma_start(rel_bc[:, slot, :], rel_pairs[pair:pair + 1, :].to_broadcast([P, 2 * GROUP])
                             ).then_inc(e_rel[slot], 16)

            sp.wait_ge(r_rel, 16)
            for pair in range(EA_RING):
                load_pair(pair)
            for i in range(Q_STAGES):
                sp.wait_ge(t_rest, 3 * i + 3)
                sp.dma_start(q_store[:, i * Q_STAGE:(i + 1) * Q_STAGE, :],
                             q_parts[:, i % Q_BUFFERS].rearrange("p t c d -> p t (c d)")
                             ).then_inc(d_q[i % Q_BUFFERS], 16)
            path = path_of(sp)
            def load_window(group):
                base = base_of(sp, group)
                slot = group % QWIN_RING
                if group >= QWIN_RING:
                    sp.wait_ge(e_q, group - QWIN_RING + 1)
                sp.dma_start(q_win[:, slot, :], q_table[bass.ds(base, P), :]).then_inc(e_qwin[slot], 16)

            def store_result(step):
                slot = step % FINAL_RING
                sp.wait_ge(f_y, step + 1)
                for tile, n, rows in stores_of(step):
                    first = (step * FINAL_TILES + tile) * P
                    sp.dma_start(out[first:first + (n - 1) * P + rows, :].rearrange("(t p) d -> p t d", p=rows),
                                 y[0:rows, slot, tile:tile + n, :]).then_inc(f_out[slot], 16)

            def all_stored():
                for slot in range(FINAL_RING):
                    sp.wait_ge(f_out[slot], 16 * sum(len(stores_of(s)) for s in range(slot, STEPS, FINAL_RING)))

            def windowed(streamed):
                for i in range(Q_BUFFERS):
                    sp.wait_ge(d_q[i], 16 * len(range(i, Q_STAGES, Q_BUFFERS)))
                stored = 0
                ahead = QWIN_RING - 2
                for group in range(ahead):
                    load_window(group)
                for pair in range(PAIRS):
                    if pair + EA_RING < PAIRS:
                        load_pair(pair + EA_RING)
                    for group in range(2 * pair + ahead, min(2 * pair + ahead + 2, GROUPS)):
                        load_window(group)
                    while (streamed and stored < STREAMED_STEPS
                           and FINISHED_AFTER[stored] + LAG_NORMALISE < 2 * pair - 3):
                        store_result(stored)
                        stored += 1
                for step in range(stored, STEPS):
                    store_result(step)
                all_stored()

            def general():
                for slot in range(EA_RING):
                    sp.wait_ge(e_ea[slot], 16)
                    sp.wait_ge(e_rel[slot], 16)
                with sp.Fori(0, GROUPS) as group:
                    sp.wait_ge(g_free, group + 1)
                    sp.dma_start(ea[0:DIM, 0, 0:GROUP], eaT[:, bass.ds(group * GROUP, GROUP)]).then_inc(g_ea, 16)
                for step in range(STEPS):
                    store_result(step)
                all_stored()

            by_path(sp, path, windowed, general)

        @block.gpsimd
        def _(pool):
            nc.gpsimd.memset(ident[:], 0.0).then_inc(c_id0, 1)
            pool.wait_ge(c_id0, 1)
            nc.gpsimd.affine_select(out=ident[:], in_=ident[:], compare_op=ALU.not_equal, fill=1.0, base=0,
                                    pattern=[[-1, P]], channel_multiplier=1).then_inc(c_ident, 1)
            nc.gpsimd.iota(iota_i[:], pattern=[[1, SPAN]], base=0, channel_multiplier=0).then_inc(c_iota, 1)
            nc.gpsimd.iota(part_i[:], pattern=[[1, 1]], base=0, channel_multiplier=1).then_inc(c_iota, 1)

            def gather(rows, table, group, t, semaphore):
                tile = group * GROUP_TILES + t
                pool.indirect_dma_start(rows, None, table,
                                        bass.IndirectOffsetOnAxis(ap=src_idx[:, tile:tile + 1], axis=0)
                                        ).then_inc(semaphore, 16)

            pool.wait_ge(l_src_early, 16)
            for group in range(EARLY):
                for t in range(GROUP_TILES):
                    gather(kv[:, group, t, 0:DIM], x_rows, group, t, e_kv[group])
            pool.wait_ge(l_src, 16)
            for i in range(2):
                pool.wait_ge(d_kv[i], 16 * len(range(i, KV_STAGES, 2)))
            path = path_of(pool)

            def windowed(streamed):
                for group in range(EARLY, GROUPS):
                    slot = group % KV_RING
                    if group >= KV_RING:
                        pool.wait_ge(e_msg, group - KV_RING + 1)
                    for t in range(tiles_of(group)):
                        gather(kv[:, slot, t, :], kv_table, group, t, e_kv[slot])

            def general():
                for i in range(Q_BUFFERS):
                    pool.wait_ge(d_q[i], 16 * len(range(i, Q_STAGES, Q_BUFFERS)))
                pool.wait_ge(l_dst, 16)
                pool.wait_ge(x_kv, 2 * EARLY)
                with pool.Fori(0, GROUPS) as group:
                    pool.wait_ge(g_free, group + 1)
                    cols = bass.ds(group * GROUP_TILES, GROUP_TILES)
                    nc.gpsimd.tensor_copy(g_src[:], src_idx[:, cols]).then_inc(g_idx, 1)
                    nc.gpsimd.tensor_copy(g_dst[:], dst_idx[:, cols]).then_inc(g_idx, 1)
                    pool.wait_ge(g_idx, group * 2 + 2)
                    pool.sem_inc(g_step, 1)
                    for t in range(GROUP_TILES):
                        pool.indirect_dma_start(
                            kv[:, 0, t, :], None, kv_table,
                            bass.IndirectOffsetOnAxis(ap=g_src[:, t:t + 1], axis=0)).then_inc(g_gather, 16)
                        pool.indirect_dma_start(
                            g_q[:, t, :], None, q_table,
                            bass.IndirectOffsetOnAxis(ap=g_dst[:, t:t + 1], axis=0)).then_inc(g_gather, 16)

            by_path(pool, path, windowed, general)

        @block.scalar
        def _(act):
            act.dma_start(rows_i[:], dst_rows).then_inc(l_rows, 16)
            act.dma_start(x_t[DIM:DIM + 1, :], ones[0:1, :]).then_inc(c_xones, 16)
            act.dma_start(dst_idx[:], dst_cols).then_inc(l_dst, 16)
            act.dma_start(early_t[DIM:DIM + 1, :, :], ones[0:1, 0:2 * GROUP]).then_inc(c_ones, 16)
            act.dma_start(ea[DIM:DIM + 1, :, :], ones[0:1, 0:EA_RING * 2 * GROUP]).then_inc(c_ones, 16)
            for pair in range(TABLE_TILES // 2):
                stage, t = divmod(2 * pair, KV_STAGE)
                if stage >= 2 and t == 0:
                    act.wait_ge(d_kv[stage % 2], 16 * (stage // 2))
                act.wait_ge(t_mm, pair + 1)
                nc.scalar.copy(kv_stage[:, stage % 2, t:t + 2, :],
                               ps_table_kv[pair % 4][:, 0:4 * DIM].rearrange("p (t d) -> p t d", t=2)
                               ).then_inc(t_kv, 1)

            def early_kv(group):
                for half in range(2):
                    act.wait_ge(x_mm, 2 * group + half + 1)
                    nc.scalar.copy(kv[:, group, 2 * half:2 * half + 2, :],
                                   ps_table_kv[(2 * group + half) % 4][:, 0:4 * DIM].rearrange(
                                       "p (t d) -> p t d", t=2)).then_inc(x_kv, 1)

            for stage in range(Q_STAGES):
                act.wait_ge(t_mq, stage + 1)
                if stage >= 2:
                    act.wait_ge(t_rest, 3 * (stage - 2) + 1)
                if stage >= Q_BUFFERS:
                    act.wait_ge(d_q[stage % Q_BUFFERS], 16 * (stage // Q_BUFFERS))
                scaled_q = ps_table_q[stage % 2][:, 0:Q_STAGE * DIM].rearrange("p (t d) -> p t d", d=DIM)
                for q in (q_full[:, stage % 2], q_parts[:, stage % Q_BUFFERS, :, 0, :]):
                    nc.scalar.mul(q, scaled_q, float(HEAD_DIM) ** -0.5).then_inc(t_q, 1)
                if 0 <= stage - 2 < EARLY:
                    early_kv(stage - 2)
            act.wait_ge(c_float, 2)
            path = path_of(act)

            def load_x_by_node(part):
                tiles = slice(part * TABLE_TILES // X_PARTS, (part + 1) * TABLE_TILES // X_PARTS)
                act.dma_start(x_n[:, tiles, :], x_rows.rearrange("(t p) d -> p t d", p=P)[:, tiles, :]
                              ).then_inc(l_xn, 16)

            def make_pick_t(group):
                pair, half, n = group // 2, group % 2, tiles_of(group) * P
                slot, b = pair % REL_RING, group % 2
                act.wait_ge(e_rel[slot], 16 * (pair // REL_RING + 1))
                if group >= 2:
                    act.wait_ge(e_pt, group - 1)
                nc.scalar.activation(distance[:, b, 0:n], rel_bc[:, slot, half * GROUP:half * GROUP + n], ACT.Abs,
                                     bias=neg_part[:]).then_inc(e_dist, 1)
                act.wait_ge(e_dist, group + 1)
                if group >= 3:
                    act.wait_ge(e_q, group - 2)
                nc.scalar.activation(pick_t[:, group % 3, 0:n], distance[:, b, 0:n], ACT.Relu,
                                     bias=1.0, scale=-1.0).then_inc(e_pt, 1)

            def exponentials(group):
                n = tiles_of(group)
                act.wait_ge(e_clip, group + 1)
                if group >= MSG_RING:
                    act.wait_ge(e_seg, group - MSG_RING + 1)
                nc.scalar.activation(msg[:, group % MSG_RING, 0:n, DIM:SUMS], clipped[:, group % 2, 0:n, :], ACT.Exp
                                     ).then_inc(e_exp, 1)

            def squares(step):
                s, n = step % FINAL_RING, tiles_in(step)
                act.wait_ge(f_mean, 2 * step + 2)
                if step >= FINAL_RING:
                    act.wait_ge(f_out[s], 16 * stores_before(step))
                for t in range(n):
                    nc.scalar.activation(y[:, s, t, :], h[:, s, t, :], ACT.Square, bias=neg_mean[:, s, t:t + 1],
                                         accum_out=var[:, s, t:t + 1]).then_inc(f_var, 1)
                act.wait_ge(f_var, step * FINAL_TILES + n)
                nc.scalar.activation(std[:, s, 0:n], var[:, s, 0:n], ACT.Sqrt,
                                     bias=eps_norm[:], scale=1.0 / DIM).then_inc(f_std, 1)

            def windowed(streamed):
                make_pick_t(0)
                make_pick_t(1)
                for group in range(GROUPS):
                    if group + 2 < GROUPS:
                        make_pick_t(group + 2)
                    exponentials(group)
                    part, between = divmod(group - X_PARTS_FROM, X_PARTS_EVERY)
                    if 0 <= part < X_PARTS and between == 0:
                        load_x_by_node(part)
                    for step in steps_at(group, LAG_SQUARE, streamed):
                        squares(step)
                nc.scalar.activation(sqrt_eps[:], eps_norm[:], ACT.Sqrt)
                for step in steps_left(streamed):
                    squares(step)

            def general():
                for part in range(X_PARTS):
                    load_x_by_node(part)
                with act.Fori(0, GROUPS) as group:
                    act.wait_ge(g_clip, group + 1)
                    nc.scalar.activation(msg[:, 0, :, DIM:SUMS], clipped[:, 0], ACT.Exp).then_inc(g_exp, 1)
                for step in range(STEPS):
                    squares(step)

            by_path(act, path, windowed, general)

        @block.vector
        def _(dve):
            dve.wait_ge(l_rows, 16)
            nc.vector.tensor_copy(rows_f, rows_i[:]).then_inc(r_chain, 1)
            dve.wait_ge(r_chain, 1)
            nc.vector.tensor_reduce(row_min[:], rows_f, axis=AX_X, op=ALU.min).then_inc(r_chain, 1)
            nc.vector.tensor_reduce(row_max[:], rows_f, axis=AX_X, op=ALU.max).then_inc(r_chain, 1)
            dve.wait_ge(r_chain, 3)
            nc.vector.tensor_tensor(row_span[:], row_max[:], row_min[:], ALU.subtract).then_inc(r_chain, 1)
            for j in range(2):
                nc.vector.tensor_scalar(rows_rel[:, j, :], rows_f[:, j, :], row_min[:, j:j + 1], None,
                                        ALU.subtract).then_inc(r_chain, 1)
            dve.wait_ge(c_iota, 2)
            nc.vector.tensor_copy(iota[:], iota_i[:]).then_inc(r_cols, 1)
            nc.vector.tensor_scalar(neg_part[:], part_i[:], -1.0, None, ALU.mult).then_inc(c_float, 1)
            nc.vector.memset(eps_norm[:], EPS_NORM).then_inc(c_float, 1)
            dve.wait_ge(l_dst, 16)
            nc.vector.tensor_copy(dst_f[:], dst_idx[:]).then_inc(r_cols, 1)
            dve.wait_ge(r_chain, 6)
            nc.vector.memset(acc_t[:], 0.0).then_inc(c_acc, 1)
            dve.wait_ge(r_load, 32)
            nc.vector.tensor_copy(base_i[:], base_all[0:1, :]).then_inc(r_cols, 1)
            nc.vector.tensor_reduce(span_max[:], span_row[:], axis=AX_X, op=ALU.max).then_inc(r_cols, 1)
            for step in range(STREAMED_STEPS):
                nc.vector.tensor_reduce(least_after[:, step:step + 1], base_all[0:1, FINISHED_AFTER[step] + 1:GROUPS],
                                        axis=AX_X, op=ALU.min).then_inc(r_cols, 1)
            dve.wait_ge(r_cols, 4 + STREAMED_STEPS)
            nc.vector.tensor_scalar(fits[:], span_max[:], float(WINDOW), None, ALU.is_lt).then_inc(r_cols, 1)
            nc.vector.tensor_scalar(step_end[:], iota[0:1, 1:1 + STREAMED_STEPS], float(STEP_NODES), None, ALU.mult
                                    ).then_inc(r_cols, 1)
            dve.wait_ge(r_cols, 6 + STREAMED_STEPS)
            nc.vector.tensor_tensor(room[:], least_after[:], step_end[:], ALU.subtract).then_inc(r_cols, 1)
            dve.wait_ge(r_cols, 7 + STREAMED_STEPS)
            nc.vector.tensor_reduce(room_min[:], room[:], axis=AX_X, op=ALU.min).then_inc(r_cols, 1)
            dve.wait_ge(r_cols, 8 + STREAMED_STEPS)
            nc.vector.tensor_scalar(streams[:], room_min[:], 0.0, 1.0, ALU.is_ge, ALU.add).then_inc(r_cols, 1)
            dve.wait_ge(r_cols, 9 + STREAMED_STEPS)
            nc.vector.tensor_tensor(path_i[:], fits[:], streams[:], ALU.mult).then_inc(r_cols, 1)
            nc.vector.tensor_tensor(
                rel_f[:].rearrange("p (n t) -> p n t", t=GROUP_TILES),
                dst_f[:].rearrange("p (n t) -> p n t", t=GROUP_TILES),
                base_all[:].unsqueeze(2).to_broadcast([P, GROUPS, GROUP_TILES]), ALU.subtract).then_inc(r_cols, 1)
            dve.wait_ge(r_cols, 11 + STREAMED_STEPS)
            dve.sem_inc(r_ready, 1)
            dve.wait_ge(c_ones, 32)

            def other_parts(stage):
                buffer, rest = q_parts[:, stage % Q_BUFFERS], q_rest[:, stage % 2]
                dve.wait_ge(t_q, 2 * stage + 2)
                if stage >= 2:
                    dve.wait_ge(t_rest, 3 * (stage - 2) + 3)
                nc.vector.tensor_tensor(rest, q_full[:, stage % 2], buffer[:, :, 0, :], ALU.subtract
                                        ).then_inc(t_rest, 1)
                dve.wait_ge(t_rest, 3 * stage + 1)
                nc.vector.tensor_copy(buffer[:, :, 1, :], rest).then_inc(t_rest, 1)
                dve.wait_ge(t_rest, 3 * stage + 2)
                nc.vector.tensor_tensor(buffer[:, :, 2, :], rest, buffer[:, :, 1, :], ALU.subtract
                                        ).then_inc(t_rest, 1)

            def early_copy(group):
                dve.wait_ge(x_tr, group + 1)
                if group >= 2:
                    dve.wait_ge(x_mm, 2 * (group - 2) + 2)
                nc.vector.tensor_copy(early_t[0:DIM, group % 2, :], ps_early_t[group % 2][0:DIM, :]
                                      ).then_inc(x_copy, 1)

            for stage in range(Q_STAGES):
                if 0 <= stage - 1 < EARLY:
                    early_copy(stage - 1)
                other_parts(stage)
            dve.wait_ge(c_acc, 1)
            path = path_of(dve)

            def make_pick(group):
                n = tiles_of(group)
                if group >= PICK_RING:
                    dve.wait_ge(e_seg, group - PICK_RING + 1)
                rel = rel_f[:, group * GROUP_TILES:group * GROUP_TILES + n]
                nc.vector.tensor_tensor(pick[:, group % PICK_RING, 0:n, :],
                                        iota[:, 0:WINDOW].unsqueeze(1).to_broadcast([P, n, WINDOW]),
                                        rel.unsqueeze(2).to_broadcast([P, n, WINDOW]), ALU.is_equal
                                        ).then_inc(e_pick, 1)

            def k_times_q(group):
                n, slot = tiles_of(group), group % KV_RING
                fetched = sum(tiles_of(g) for g in range(slot, group + 1, KV_RING))
                dve.wait_ge(e_kv[slot], 16 * fetched)
                if group < EARLY:
                    dve.wait_ge(x_kv, 2 * group + 2)
                dve.wait_ge(e_q, group + 1)
                if group >= 2:
                    dve.wait_ge(e_kqe, group - 1)
                nc.vector.tensor_tensor(kq[:, group % 2, 0:n, :], kv[:, slot, 0:n, 0:DIM],
                                        ps_q[group % 2][:, 0:n * DIM].rearrange("p (t d) -> p t d", t=n),
                                        ALU.mult).then_inc(e_kq, 1)

            def times_e(group):
                n = tiles_of(group)
                dve.wait_ge(e_kq, group + 1)
                dve.wait_ge(e_e, group + 1)
                nc.vector.tensor_tensor(kqe[:, group % 2, 0:n, :], kq[:, group % 2, 0:n, :],
                                        ps_e[group % 2][:, 0:n * DIM].rearrange("p (t d) -> p t d", t=n),
                                        ALU.mult).then_inc(e_kqe, 1)

            def sum_heads(group):
                n = tiles_of(group)
                dve.wait_ge(e_kqe, group + 1)
                nc.vector.tensor_reduce(score[:, group % 2, 0:n, :],
                                        kqe[:, group % 2, 0:n, :].rearrange("p t (h d) -> p t h d", h=HEADS),
                                        axis=AX_X, op=ALU.add).then_inc(e_sum, 1)

            def clip(group):
                n = tiles_of(group)
                dve.wait_ge(e_sum, group + 1)
                if group >= 2:
                    dve.wait_ge(e_exp, group - 1)
                nc.vector.tensor_scalar(clipped[:, group % 2, 0:n, :], score[:, group % 2, 0:n, :],
                                        CLIP, -CLIP, ALU.min, ALU.max).then_inc(e_clip, 1)

            def weigh_v(group):
                n = tiles_of(group)
                dve.wait_ge(e_exp, group + 1)
                m = msg[:, group % MSG_RING, 0:n, :]
                nc.vector.tensor_tensor(
                    m[:, :, 0:DIM].rearrange("p t (h d) -> p t h d", h=HEADS),
                    kv[:, group % KV_RING, 0:n, DIM:2 * DIM].rearrange("p t (h d) -> p t h d", h=HEADS),
                    m[:, :, DIM:SUMS].unsqueeze(3).to_broadcast([P, n, HEADS, HEAD_DIM]), ALU.mult
                ).then_inc(e_msg, 1)

            def accumulate(group):
                base = base_of(dve, group)
                dve.wait_ge(e_seg, group + 1)
                if group:
                    dve.wait_ge(e_acc, group)
                window = acc_t[:, bass.ds(base, WINDOW)]
                nc.vector.tensor_tensor(window, window, ps_seg[group % 2][0:SUMS, 0:WINDOW], ALU.add
                                        ).then_inc(e_acc, 1)

            def heads(a):
                return a.rearrange("p t (h d) -> p t h d", h=HEADS)

            def divide(step):
                first, n, s = step * FINAL_TILES, tiles_in(step), step % FINAL_RING
                sums = ps_node[step % 2][:, 0:n * SUMS].rearrange("p (t c) -> p t c", t=n)
                dve.wait_ge(f_tr, step + 1)
                nc.vector.tensor_scalar(z_eps[:, s, 0:n, :], sums[:, :, DIM:SUMS], EPS_Z, None, ALU.add
                                        ).then_inc(f_z, 1)
                dve.wait_ge(f_z, 2 * step + 1)
                nc.vector.reciprocal(z_inv[:, s, 0:n, :], z_eps[:, s, 0:n, :]).then_inc(f_z, 1)
                dve.wait_ge(f_z, 2 * step + 2)
                if step >= FINAL_RING:
                    dve.wait_ge(f_y, step - FINAL_RING + 1)
                nc.vector.tensor_tensor(heads(h[:, s, 0:n, :]), heads(sums[:, :, 0:DIM]),
                                        z_inv[:, s, 0:n, :].unsqueeze(3).to_broadcast([P, n, HEADS, HEAD_DIM]),
                                        ALU.mult).then_inc(f_div, 1)
                dve.wait_ge(f_div, step + 1)
                nc.vector.tensor_tensor(h[:, s, 0:n, :], h[:, s, 0:n, :], x_n[:, first:first + n, :], ALU.add
                                        ).then_inc(f_hx, 1)
                dve.wait_ge(f_hx, step + 1)
                nc.vector.tensor_reduce(total[:, s, 0:n], h[:, s, 0:n, :], axis=AX_X, op=ALU.add
                                        ).then_inc(f_mean, 1)
                dve.wait_ge(f_mean, 2 * step + 1)
                nc.vector.tensor_scalar(neg_mean[:, s, 0:n], total[:, s, 0:n], -1.0 / DIM, None, ALU.mult
                                        ).then_inc(f_mean, 1)

            def normalise(step):
                n, s = tiles_in(step), step % FINAL_RING
                dve.wait_ge(f_std, step + 1)
                nc.vector.reciprocal(rstd[:, s, 0:n], std[:, s, 0:n]).then_inc(f_rstd, 1)
                dve.wait_ge(f_rstd, step + 1)
                for t in range(n):
                    last = nc.vector.tensor_scalar(y[:, s, t, :], h[:, s, t, :], neg_mean[:, s, t:t + 1],
                                                   rstd[:, s, t:t + 1], ALU.add, ALU.mult)
                last.then_inc(f_y, 1)

            def finish_nodes(steps):
                dve.wait_ge(l_xn, 16 * X_PARTS)
                for step in steps:
                    divide(step)
                    if step > steps[0]:
                        normalise(step - 1)
                normalise(steps[-1])

            def windowed(streamed):
                for i in range(2):
                    dve.wait_ge(d_kv[i], 16 * len(range(i, KV_STAGES, 2)))
                dve.wait_ge(t_rest, 3 * Q_STAGES)
                make_pick(0)
                for group in range(GROUPS + 2):
                    if group == GROUPS:
                        weigh_v(group - 1)
                    if group < GROUPS:
                        k_times_q(group)
                    if group + 1 < GROUPS:
                        make_pick(group + 1)
                    if group < GROUPS:
                        times_e(group)
                    if 2 <= group:
                        accumulate(group - 2)
                    if group < GROUPS:
                        sum_heads(group)
                    if 1 <= group < GROUPS:
                        weigh_v(group - 1)
                    if group < GROUPS:
                        clip(group)
                    if streamed and group == FINISHED_AFTER[0]:
                        dve.wait_ge(l_xn, 16 * X_PARTS)
                    for step in steps_at(group, LAG_DIVIDE, streamed):
                        divide(step)
                    for step in steps_at(group, LAG_NORMALISE, streamed):
                        normalise(step)
                finish_nodes(steps_left(streamed))

            def general():
                for i in range(2):
                    dve.wait_ge(d_kv[i], 16 * len(range(i, KV_STAGES, 2)))
                dve.wait_ge(x_kv, 2 * EARLY)
                dve.sem_inc(g_free, 1)
                per_group = 8 + SPANS
                with dve.Fori(0, GROUPS) as group:
                    done = [0]

                    def then(instruction):
                        done[0] += 1
                        instruction.then_inc(g_chain, 1)
                        dve.wait_ge(g_chain, group * per_group + done[0])

                    cols = bass.ds(group * GROUP_TILES, GROUP_TILES)
                    then(nc.vector.tensor_copy(g_dst_f[:], dst_f[:, cols]))
                    dve.wait_ge(g_gather, group * (32 * GROUP_TILES) + 32 * GROUP_TILES)
                    q, part = kq[:, 1], [g_q[:, :, c * DIM:(c + 1) * DIM] for c in range(PARTS)]
                    then(nc.vector.tensor_tensor(q, part[0], part[1], ALU.add))
                    then(nc.vector.tensor_tensor(q, q, part[2], ALU.add))
                    then(nc.vector.tensor_tensor(kq[:, 0], q, kv[:, 0, :, 0:DIM], ALU.mult))
                    dve.wait_ge(g_e, group + 1)
                    then(nc.vector.tensor_tensor(kqe[:, 0], kq[:, 0], ps_e[0][:, 0:GROUP_TILES * DIM].rearrange(
                        "p (t d) -> p t d", t=GROUP_TILES), ALU.mult))
                    then(nc.vector.tensor_reduce(score[:, 0], heads(kqe[:, 0]), axis=AX_X, op=ALU.add))
                    then(nc.vector.tensor_scalar(clipped[:, 0], score[:, 0], CLIP, -CLIP, ALU.min, ALU.max))
                    dve.sem_inc(g_clip, 1)
                    dve.wait_ge(g_exp, group + 1)
                    m = msg[:, 0]
                    then(nc.vector.tensor_tensor(
                        heads(m[:, :, 0:DIM]), heads(kv[:, 0, :, DIM:2 * DIM]),
                        m[:, :, DIM:SUMS].unsqueeze(3).to_broadcast([P, GROUP_TILES, HEADS, HEAD_DIM]), ALU.mult))
                    for span in range(SPANS):
                        for t in range(GROUP_TILES):
                            last = nc.vector.tensor_scalar(g_pick[:, t, :], iota[:], float(span * SPAN),
                                                           g_dst_f[:, t:t + 1], ALU.add, ALU.is_equal)
                        last.then_inc(g_pk, 1)
                        dve.wait_ge(g_seg, group * SPANS + (span + 1))
                        nodes = acc_t[:, span * SPAN:(span + 1) * SPAN]
                        then(nc.vector.tensor_tensor(nodes, nodes, ps_seg[0][0:SUMS, :], ALU.add))
                    dve.sem_inc(g_free, 1)
                dve.sem_inc(g_acc, 1)
                finish_nodes(range(STEPS))

            by_path(dve, path, windowed, general)

        @block.tensor
        def _(pe):
            pe.wait_ge(c_xones, 16)
            pe.wait_ge(l_w, 32)
            for tile in range(TABLE_TILES):
                pair, half = divmod(tile, 2)
                if tile % KV_STAGE == 0:
                    pe.wait_ge(l_x[tile // KV_STAGE], 16)
                if half == 0 and pair >= 4:
                    pe.wait_ge(t_kv, pair - 3)
                last = nc.tensor.matmul(ps_table_kv[pair % 4][:, half * 2 * DIM:(half + 1) * 2 * DIM],
                                        x_t[:, tile * P:(tile + 1) * P], w_kv, start=True, stop=True)
                if half == 1:
                    last.then_inc(t_mm, 1)
            pe.wait_ge(c_ident, 1)

            def stage_of_q(stage):
                if stage >= 2:
                    pe.wait_ge(t_q, 2 * (stage - 1))
                for t in range(Q_STAGE):
                    tile = stage * Q_STAGE + t
                    last = nc.tensor.matmul(ps_table_q[stage % 2][:, t * DIM:(t + 1) * DIM],
                                            x_t[:, tile * P:(tile + 1) * P], w_q, start=True, stop=True)
                last.then_inc(t_mq, 1)

            def early_transpose(group):
                pe.wait_ge(e_kv[group], 16 * GROUP_TILES)
                if group >= 2:
                    pe.wait_ge(x_copy, group - 1)
                for t in range(GROUP_TILES):
                    last = nc.tensor.transpose(ps_early_t[group % 2][0:DIM, t * P:(t + 1) * P],
                                               kv[:, group, t, 0:DIM], ident[:])
                last.then_inc(x_tr, 1)

            def early_products(group):
                pe.wait_ge(x_copy, group + 1)
                for half in range(2):
                    if 2 * group + half >= 4:
                        pe.wait_ge(x_kv, 2 * group + half - 3)
                    for j in range(2):
                        t = 2 * half + j
                        last = nc.tensor.matmul(ps_table_kv[(2 * group + half) % 4][:, j * 2 * DIM:(j + 1) * 2 * DIM],
                                                early_t[:, group % 2, t * P:(t + 1) * P], w_kv,
                                                start=True, stop=True)
                    last.then_inc(x_mm, 1)

            for stage in range(Q_STAGES):
                stage_of_q(stage)
                if 0 <= stage - 1 < EARLY:
                    early_transpose(stage - 1)
                if stage == 2:
                    pe.wait_ge(t_kv, TABLE_TILES // 2)
                if 0 <= stage - 2 < EARLY:
                    early_products(stage - 2)
            pe.wait_ge(x_kv, 2 * EARLY)
            pe.wait_ge(t_q, 2 * Q_STAGES)
            pe.wait_ge(c_ones, 32)
            path = path_of(pe)

            def edge_features(group):
                pair, half = group // 2, group % 2
                slot = pair % EA_RING
                pe.wait_ge(e_ea[slot], 16 * (pair // EA_RING + 1))
                if group >= 2:
                    pe.wait_ge(e_kqe, group - 1)
                for t in range(tiles_of(group)):
                    at = half * GROUP + t * P
                    last = nc.tensor.matmul(ps_e[group % 2][:, t * DIM:(t + 1) * DIM], ea[:, slot, at:at + P],
                                            w_e, start=True, stop=True)
                last.then_inc(e_e, 1)

            def edge_queries(group):
                slot = group % QWIN_RING
                pe.wait_ge(e_qwin[slot], 16 * (group // QWIN_RING + 1))
                pe.wait_ge(e_pt, group + 1)
                if group >= 2:
                    pe.wait_ge(e_kq, group - 1)
                for t in range(tiles_of(group)):
                    for part in range(PARTS):
                        last = nc.tensor.matmul(ps_q[group % 2][:, t * DIM:(t + 1) * DIM],
                                                pick_t[:, group % 3, t * P:(t + 1) * P],
                                                q_win[:, slot, part * DIM:(part + 1) * DIM],
                                                start=(part == 0), stop=(part == PARTS - 1))
                last.then_inc(e_q, 1)

            def segment_sums(group):
                n = tiles_of(group)
                pe.wait_ge(e_pick, group + 1)
                pe.wait_ge(e_msg, group + 1)
                if group >= 2:
                    pe.wait_ge(e_acc, group - 1)
                for t in range(n):
                    last = nc.tensor.matmul(ps_seg[group % 2][0:SUMS, 0:WINDOW], msg[:, group % MSG_RING, t, :],
                                            pick[:, group % PICK_RING, t, :], start=(t == 0), stop=(t == n - 1))
                last.then_inc(e_seg, 1)

            def sums_by_node(step):
                if step >= 2:
                    pe.wait_ge(f_div, step - 1)
                for t in range(tiles_in(step)):
                    tile = step * FINAL_TILES + t
                    last = nc.tensor.transpose(ps_node[step % 2][:, t * SUMS:(t + 1) * SUMS],
                                               acc_t[:, tile * P:(tile + 1) * P], ident[0:SUMS, 0:SUMS])
                last.then_inc(f_tr, 1)

            def windowed(streamed):
                edge_features(0)
                edge_queries(0)
                for group in range(GROUPS + 1):
                    if group + 1 < GROUPS:
                        edge_features(group + 1)
                        edge_queries(group + 1)
                    if group >= 1:
                        segment_sums(group - 1)
                    for step in steps_at(group, LAG_TRANSPOSE, streamed):
                        pe.wait_ge(e_acc, FINISHED_AFTER[step] + 1)
                        sums_by_node(step)
                pe.wait_ge(e_acc, GROUPS)
                for step in steps_left(streamed):
                    sums_by_node(step)

            def general():
                with pe.Fori(0, GROUPS) as group:
                    pe.wait_ge(g_ea, group * 16 + 16)
                    for t in range(GROUP_TILES):
                        last = nc.tensor.matmul(ps_e[0][:, t * DIM:(t + 1) * DIM], ea[:, 0, t * P:(t + 1) * P],
                                                w_e, start=True, stop=True)
                    last.then_inc(g_e, 1)
                    for span in range(SPANS):
                        pe.wait_ge(g_pk, group * SPANS + (span + 1))
                        for t in range(GROUP_TILES):
                            last = nc.tensor.matmul(ps_seg[0][0:SUMS, :], msg[:, 0, t, :], g_pick[:, t, :],
                                                    start=(t == 0), stop=(t == GROUP_TILES - 1))
                        last.then_inc(g_seg, 1)
                pe.wait_ge(g_acc, 1)
                for step in range(STEPS):
                    sums_by_node(step)

            by_path(pe, path, windowed, general)


def kernel(x, src, dst, edge_attr_96, L0_gnn_Wq, L0_gnn_bq, L0_gnn_Wk, L0_gnn_bk, L0_gnn_We, L0_gnn_be,
           L0_gnn_Wv, L0_gnn_bv):
    import concourse.bacc as bacc
    from concourse.bass_utils import run_bass_kernel_spmd

    x, src, dst, edge_attr = (np.asarray(a) for a in (x, src, dst, edge_attr_96))
    x_rows = np.zeros((TABLE_ROWS, DIM), x.dtype)
    x_rows[:N_NODES] = x
    ea_t = np.zeros((DIM, EDGES_PADDED), edge_attr.dtype)
    ea_t[:, :N_EDGES] = edge_attr.T
    src_padded = np.zeros(EDGES_PADDED, src.dtype)
    src_padded[:N_EDGES] = src
    dst_padded = np.full(EDGES_PADDED, N_NODES, dst.dtype)
    dst_padded[:N_EDGES] = dst

    arrays = {
        "x_t_in": np.ascontiguousarray(x_rows.T),
        "x_rows_in": x_rows,
        "src_cols_in": np.ascontiguousarray(src_padded.reshape(-1, P).T).view(np.uint32),
        "dst_cols_in": np.ascontiguousarray(dst_padded.reshape(-1, P).T).view(np.uint32),
        "dst_rows_in": dst_padded.reshape(PAIRS, 2, GROUP),
        "ea_t_in": ea_t,
    }
    arrays["weights_in"] = np.concatenate([L0_gnn_Wk, L0_gnn_Wv, L0_gnn_Wq, L0_gnn_We], axis=1)
    arrays["biases_in"] = np.concatenate([L0_gnn_bk, L0_gnn_bv, L0_gnn_bq, L0_gnn_be]).reshape(1, 4 * DIM)

    arrays["ones_in"] = np.ones((1, TABLE_ROWS), np.float32)

    nc = bacc.Bacc("TRN2", target_bir_lowering=False, num_devices=1)
    ap = {n: nc.dram_tensor(n, a.shape, mybir.dt.from_np(a.dtype), kind="ExternalInput").ap()
          for n, a in arrays.items()}
    out = nc.dram_tensor("out", [N_NODES, DIM], F32, kind="ExternalOutput").ap()
    build(nc, ap["x_t_in"], ap["x_rows_in"], ap["src_cols_in"], ap["dst_cols_in"], ap["dst_rows_in"],
          ap["ea_t_in"], ap["weights_in"], ap["biases_in"], ap["ones_in"], out)
    r = run_bass_kernel_spmd(nc, [arrays], core_ids=[0])
    return r.results[0]["out"]
```
